# Optimizing a Trainium2 kernel written in Bass

```python
import numpy as np
import jax
import jax.numpy as jnp

def _softmax(x, axis=-1):
    return jax.nn.softmax(x, axis=axis)

def _gelu(x):
    return jax.nn.gelu(x, approximate=True)

def _silu(x):
    return jax.nn.silu(x)

def _sigmoid(x):
    return jax.nn.sigmoid(x)

def _layernorm(x, axis=-1, eps=1e-05):
    m = jnp.mean(x, axis=axis, keepdims=True)
    v = jnp.var(x, axis=axis, keepdims=True)
    return (x - m) / jnp.sqrt(v + eps)

def _scatter_add(tgt, idx, src, axis=0):
    return tgt.at[idx].add(src)

def _segment_sum(src, seg, n):
    return jax.ops.segment_sum(src, seg, n)
kernel_name = 'mk_adj_resnorm_d4_adj_r2_8d1ede'

def setup_inputs(seed: int=0):
    np.random.seed(seed)
    _w = jnp.asarray

    def _rec_inputs():
        import jax
        import jax.numpy as jnp
        _gk = jax.random.key(seed)
        x = -0.0005207 + 1.001 * jax.random.normal(jax.random.fold_in(_gk, 1), (128, 128, 128), jnp.float32)
        _a = jax.random.bernoulli(jax.random.fold_in(_gk, 2), 0.0625, (128, 128, 128))
        _a = jnp.logical_or(_a, jnp.swapaxes(_a, -1, -2))
        _a = jnp.logical_or(_a, jnp.eye(128, dtype=bool))
        _af = _a.astype(jnp.float32)
        _af = _af * jax.random.uniform(jax.random.fold_in(_gk, 3), (128, 128, 128), jnp.float32, 0.05, 1)
        adj = _af
        _nm = jnp.ones((128, 128), dtype=bool)
        nodemask = jnp.where(_nm, 1.0, 0.0).astype(jnp.float32)
        return (x, adj, nodemask)
    x, adj, nodemask = _rec_inputs()

    def _L0_gnn_setup():
        import math
        import jax, jax.numpy as jnp
        import numpy as np
        HIDDEN = 128
        HEADS = 8
        HEAD_DIM = HIDDEN // HEADS
        key = jax.random.key(seed)
        ks = jax.random.split(key, 8)
        b, n = (2, 2048)
        node_state = jax.random.normal(ks[0], (b, n, HIDDEN), dtype=jnp.float32)
        adjacency = jax.random.uniform(ks[1], (b, n, n), dtype=jnp.float32)
        s = 1.0 / math.sqrt(HIDDEN)
        Wq = jax.random.uniform(ks[2], (HIDDEN, HIDDEN), jnp.float32, -s, s)
        Wk = jax.random.uniform(ks[3], (HIDDEN, HIDDEN), jnp.float32, -s, s)
        Wv = jax.random.uniform(ks[4], (HIDDEN, HIDDEN), jnp.float32, -s, s)
        Wo = jax.random.uniform(ks[5], (HIDDEN, HIDDEN), jnp.float32, -s, s)
        bo = jax.random.uniform(ks[6], (HIDDEN,), jnp.float32, -s, s)
        return {'node_state': node_state, 'adjacency': adjacency, 'Wq': Wq, 'Wk': Wk, 'Wv': Wv, 'Wo': Wo, 'bo': bo}
    _L0_gnn_all = _L0_gnn_setup()
    _L0_gnn_in = {k: v for k, v in _L0_gnn_all.items() if k in ('Wq', 'Wk', 'Wv', 'Wo', 'bo')}
    del _L0_gnn_all

    def _L1_gnn_setup():
        import jax, jax.numpy as jnp
        import numpy as np
        B, N, D, C, L = (64, 256, 128, 128, 5)
        EDGE_P = 0.02

        def _gru_cell(m, h, w_ih, w_hh, b_ih, b_hh):
            gi = m @ w_ih.T + b_ih
            gh = h @ w_hh.T + b_hh
            i_r, i_z, i_n = jnp.split(gi, 3, axis=-1)
            h_r, h_z, h_n = jnp.split(gh, 3, axis=-1)
            r = jax.nn.sigmoid(i_r + h_r)
            z = jax.nn.sigmoid(i_z + h_z)
            n = jnp.tanh(i_n + r * h_n)
            return (1.0 - z) * n + z * h
        key = jax.random.key(seed)
        ks = jax.random.split(key, 8)
        x = jax.random.normal(ks[0], (B, N, D), dtype=jnp.float32)
        adj = (jax.random.uniform(ks[1], (B, N, N)) < EDGE_P).astype(jnp.float32)
        mask = jnp.ones((B, N), dtype=jnp.float32)
        s = 1.0 / np.sqrt(C).astype(np.float32)
        weight = jax.random.uniform(ks[2], (L, C, C), minval=-s, maxval=s, dtype=jnp.float32)
        w_ih = jax.random.uniform(ks[3], (3 * C, C), minval=-s, maxval=s, dtype=jnp.float32)
        w_hh = jax.random.uniform(ks[4], (3 * C, C), minval=-s, maxval=s, dtype=jnp.float32)
        b_ih = jax.random.uniform(ks[5], (3 * C,), minval=-s, maxval=s, dtype=jnp.float32)
        b_hh = jax.random.uniform(ks[6], (3 * C,), minval=-s, maxval=s, dtype=jnp.float32)
        return dict(x=x, adj=adj, mask=mask, weight=weight, w_ih=w_ih, w_hh=w_hh, b_ih=b_ih, b_hh=b_hh)
    _L1_gnn_all = _L1_gnn_setup()
    _L1_gnn_in = {k: v for k, v in _L1_gnn_all.items() if k in ('weight', 'w_ih', 'w_hh', 'b_ih', 'b_hh')}
    del _L1_gnn_all

    def _L2_gnn_setup():
        import jax, jax.numpy as jnp
        import numpy as np
        key = jax.random.key(seed)
        k1, k2, k3, k4 = jax.random.split(key, 4)
        B, N, d_in, d_out = (8, 1024, 128, 128)
        x = jax.random.normal(k1, (B, N, d_in), dtype=jnp.float32)
        adj_hat = jax.random.uniform(k2, (B, N, N), dtype=jnp.float32)
        W = jax.random.normal(k3, (d_out, d_in), dtype=jnp.float32) * (1.0 / np.sqrt(d_in))
        b = jax.random.normal(k4, (d_out,), dtype=jnp.float32) * 0.01
        return {'x': x, 'adj_hat': adj_hat, 'W': W, 'b': b}
    _L2_gnn_all = _L2_gnn_setup()
    _L2_gnn_in = {k: v for k, v in _L2_gnn_all.items() if k in ('W', 'b')}
    del _L2_gnn_all

    def _L3_gnn_setup():
        import jax, jax.numpy as jnp
        import numpy as np
        D_IN = 128
        D_HID = 256
        key = jax.random.key(seed)
        k1, k2, k3, k4, k5, k6 = jax.random.split(key, 6)
        x = jax.random.normal(k1, (8, 2048, D_IN), dtype=jnp.float32)
        adj = jax.random.uniform(k2, (8, 2048, 2048), dtype=jnp.float32)
        s1 = 1.0 / np.sqrt(D_IN)
        s2 = 1.0 / np.sqrt(D_HID)
        W1 = jax.random.uniform(k3, (D_IN, D_HID), dtype=jnp.float32, minval=-s1, maxval=s1)
        b1 = jax.random.uniform(k4, (D_HID,), dtype=jnp.float32, minval=-s1, maxval=s1)
        W2 = jax.random.uniform(k5, (D_HID, D_IN), dtype=jnp.float32, minval=-s2, maxval=s2)
        b2 = jax.random.uniform(k6, (D_IN,), dtype=jnp.float32, minval=-s2, maxval=s2)
        eps = jnp.zeros((1,), dtype=jnp.float32)
        return {'x': x, 'adj': adj, 'eps': eps, 'W1': W1, 'b1': b1, 'W2': W2, 'b2': b2}
    _L3_gnn_all = _L3_gnn_setup()
    _L3_gnn_in = {k: v for k, v in _L3_gnn_all.items() if k in ('eps', 'W1', 'b1', 'W2', 'b2')}
    del _L3_gnn_all
    return {'x': x, 'adj': adj, 'nodemask': nodemask, 'L0_gnn_Wq': _L0_gnn_in['Wq'], 'L0_gnn_Wk': _L0_gnn_in['Wk'], 'L0_gnn_Wv': _L0_gnn_in['Wv'], 'L0_gnn_Wo': _L0_gnn_in['Wo'], 'L0_gnn_bo': _L0_gnn_in['bo'], 'L1_gnn_weight': _L1_gnn_in['weight'], 'L1_gnn_w_ih': _L1_gnn_in['w_ih'], 'L1_gnn_w_hh': _L1_gnn_in['w_hh'], 'L1_gnn_b_ih': _L1_gnn_in['b_ih'], 'L1_gnn_b_hh': _L1_gnn_in['b_hh'], 'L2_gnn_W': _L2_gnn_in['W'], 'L2_gnn_b': _L2_gnn_in['b'], 'L3_gnn_eps': _L3_gnn_in['eps'], 'L3_gnn_W1': _L3_gnn_in['W1'], 'L3_gnn_b1': _L3_gnn_in['b1'], 'L3_gnn_W2': _L3_gnn_in['W2'], 'L3_gnn_b2': _L3_gnn_in['b2']}

def reference(x, adj, nodemask, L0_gnn_Wq, L0_gnn_Wk, L0_gnn_Wv, L0_gnn_Wo, L0_gnn_bo, L1_gnn_weight, L1_gnn_w_ih, L1_gnn_w_hh, L1_gnn_b_ih, L1_gnn_b_hh, L2_gnn_W, L2_gnn_b, L3_gnn_eps, L3_gnn_W1, L3_gnn_b1, L3_gnn_W2, L3_gnn_b2):
    import jax
    import jax.numpy as jnp

    def _L0_gnn_ref(node_state, adjacency, Wq, Wk, Wv, Wo, bo):
        import math
        import jax, jax.numpy as jnp
        import numpy as np
        HIDDEN = 128
        HEADS = 8
        HEAD_DIM = HIDDEN // HEADS
        b, n, _ = node_state.shape

        def split_heads(x):
            return x.reshape(b, n, HEADS, HEAD_DIM).transpose(0, 2, 1, 3)
        q = split_heads(node_state @ Wq.T)
        k = split_heads(node_state @ Wk.T)
        v = split_heads(node_state @ Wv.T)
        scores = jnp.einsum('bhqd,bhkd->bhqk', q, k) / math.sqrt(HEAD_DIM)
        log_adj = jnp.log(adjacency + 1e-06)
        scores = scores + log_adj[:, None, :, :]
        attn = jax.nn.softmax(scores, axis=-1)
        out = jnp.einsum('bhqk,bhkd->bhqd', attn, v)
        out = out.transpose(0, 2, 1, 3).reshape(b, n, HIDDEN)
        return out @ Wo.T + bo

    def _L1_gnn_ref(x, adj, mask, weight, w_ih, w_hh, b_ih, b_hh):
        import jax, jax.numpy as jnp
        import numpy as np
        B, N, D, C, L = (64, 256, 128, 128, 5)
        EDGE_P = 0.02

        def _gru_cell(m, h, w_ih, w_hh, b_ih, b_hh):
            gi = m @ w_ih.T + b_ih
            gh = h @ w_hh.T + b_hh
            i_r, i_z, i_n = jnp.split(gi, 3, axis=-1)
            h_r, h_z, h_n = jnp.split(gh, 3, axis=-1)
            r = jax.nn.sigmoid(i_r + h_r)
            z = jax.nn.sigmoid(i_z + h_z)
            n = jnp.tanh(i_n + r * h_n)
            return (1.0 - z) * n + z * h
        A = (adj != 0).astype(x.dtype)
        h = x
        for l in range(weight.shape[0]):
            m = jnp.einsum('bnd,de->bne', h, weight[l])
            agg = jnp.einsum('bij,bid->bjd', A, m)
            h = _gru_cell(agg, h, w_ih, w_hh, b_ih, b_hh)
        return h * mask[..., None]

    def _L2_gnn_ref(x, adj_hat, W, b):
        import jax, jax.numpy as jnp
        import numpy as np
        N = adj_hat.shape[1]
        diag = jnp.diagonal(adj_hat, axis1=-2, axis2=-1)
        d = adj_hat.sum(axis=-1) - diag
        d_inv_sqrt = jnp.power(d, -0.5)
        dad = d_inv_sqrt[:, :, None] * adj_hat * d_inv_sqrt[:, None, :]
        h = jnp.einsum('bnd,od->bno', x, W) + b
        return jnp.einsum('bnm,bmo->bno', dad, h)

    def _L3_gnn_ref(x, adj, eps, W1, b1, W2, b2):
        import jax, jax.numpy as jnp
        import numpy as np
        D_IN = 128
        D_HID = 256
        aggregated = jnp.einsum('bnm,bmd->bnd', adj, x)
        h = (1.0 + eps) * x + aggregated
        h = jax.nn.relu(h @ W1 + b1)
        return h @ W2 + b2
    x = _layernorm(x + _L0_gnn_ref(x, adj, L0_gnn_Wq, L0_gnn_Wk, L0_gnn_Wv, L0_gnn_Wo, L0_gnn_bo), axis=-1)
    x = _layernorm(x + _L1_gnn_ref(x, adj, nodemask, L1_gnn_weight, L1_gnn_w_ih, L1_gnn_w_hh, L1_gnn_b_ih, L1_gnn_b_hh), axis=-1)
    x = _layernorm(x + _L2_gnn_ref(x, adj, L2_gnn_W, L2_gnn_b), axis=-1)
    x = _layernorm(x + _L3_gnn_ref(x, adj, L3_gnn_eps, L3_gnn_W1, L3_gnn_b1, L3_gnn_W2, L3_gnn_b2), axis=-1)
    return x

_drawn_inputs = setup_inputs


def setup_inputs(seed=0):
    import zlib

    import numpy as np

    out = dict(_drawn_inputs(seed))
    spreads = {}
    factors = {'L2_gnn_b': 4.681, 'L3_gnn_b1': 4.8}
    for name, (base, spread) in spreads.items():
        noise = np.random.default_rng([zlib.crc32(name.encode()), seed]).standard_normal(out[name].shape)
        drawn = base * np.exp(spread * noise) if base else spread * noise
        out[name] = jnp.asarray(drawn.astype(out[name].dtype))
    for name, factor in factors.items():
        out[name] = (out[name] * factor).astype(out[name].dtype)
    return out
```

```python
from contextlib import ExitStack

import concourse.bass as bass
from concourse import mybir

F32 = mybir.dt.float32
ALU = mybir.AluOpType
ACT = mybir.ActivationFunctionType
AX_X = mybir.AxisListType.X

P = 128
G = 4
S = 2
W = G * P
LN_EPS = 1e-5
ADJ_EPS = 1e-6


class Signal:

    def __init__(self, sem, per_round, unit=1):
        self.sem, self.per_round, self.unit = sem, per_round, unit

    def after(self, rnd, k):
        return (rnd + 1) * (self.per_round * self.unit) + k * self.unit


def gnn_stack(nc, t, out):
    B, N, D = t["x"].shape
    assert N == P and D == P
    heads = 8
    dh = D // heads
    layers = t["L1_weight_T"].shape[0]
    rounds = B // (G * S)
    units = G * S
    half_heads = heads // 2
    pad = P // half_heads
    vw = dh + 1

    with ExitStack() as ctx:
        def sb(name, shape):
            return ctx.enter_context(nc.sbuf_tensor(name, shape, F32))

        def signal(name, per_round, unit=1):
            s = Signal(ctx.enter_context(nc.semaphore(name)), per_round, unit)
            signals.append(s)
            return s

        signals = []
        bank = [ctx.enter_context(nc.psum_tensor(f"bank{i}", [P, W], F32)) for i in range(8)]
        ps_s = [bank[0], bank[1]]
        ps_st = [bank[2], bank[3]]
        ps_o = [bank[4], bank[5]]
        ps_m = [bank[6], bank[7]]

        ident = sb("ident", [P, P])
        off_diag = sb("off_diag", [P, P])
        eps_ident = sb("eps_ident", [P, P])
        wq = sb("wq", [P, 2, half_heads, pad])
        wk = sb("wk", [P, 2, half_heads, pad])
        wv = sb("wv", [P, P])
        wo = sb("wo", [P, P])
        bo = sb("bo", [P, P])
        k_bias = sb("k_bias", [P, 1])
        w_l = sb("w_l", [P, layers, P])
        w_ih = sb("w_ih", [P, 3 * P])
        w_hh = sb("w_hh", [P, 3 * P])
        w_in = sb("w_in", [P, layers, 3 * P])
        b_ih = sb("b_ih", [P, 3])
        b_hh = sb("b_hh", [P, 3])
        b_half = sb("b_half", [P, 3])
        w2g = sb("w2g", [P, P])
        b2g = sb("b2g", [P, P])
        w31 = sb("w31", [P, 2 * P])
        b31 = sb("b31", [P, 2])
        w32 = sb("w32", [P, 2, P])
        b32 = sb("b32", [P, P])
        eps3 = sb("eps3", [P, 1])
        nodemask = sb("nodemask", [P, B])
        power = sb("power", [P, G])
        ln_eps = sb("ln_eps", [P, G])

        def per_stream(name, shape):
            return [sb(f"{name}{s}", shape) for s in range(S)]

        x_in = per_stream("x_in", [P, G, P])
        adj = per_stream("adj", [P, G, P])
        adjT = per_stream("adjT", [P, G, P])
        adj_on = per_stream("adj_on", [P, G, P])
        adj_off = per_stream("adj_off", [P, G, P])
        adj2 = per_stream("adj2", [P, G, P])
        adj3 = per_stream("adj3", [P, G, P])
        deg = per_stream("deg", [P, G])
        dis = per_stream("dis", [P, G])
        xT = per_stream("xT", [P, W])
        qT = per_stream("qT", [P, 2, W])
        kT = per_stream("kT", [P, 2, W])
        v1 = per_stream("v1", [P, G, heads, vw])
        maxima = per_stream("maxima", [P, G, 2, half_heads, pad])
        e = [sb(f"e{i}", [P, heads, P]) for i in range(2)]
        r_sum = [sb(f"r_sum{i}", [P, heads]) for i in range(2)]
        o_n = per_stream("o_n", [P, G, heads, dh])
        oT = per_stream("oT", [P, W])
        res = per_stream("res", [P, G, P])
        t_ln = per_stream("t_ln", [P, G, P])
        stats = per_stream("stats", [P, G, 6])
        mean_var = per_stream("mean_var", [P, G, 2])
        var_eps = per_stream("var_eps", [P, G])
        rstd = per_stream("rstd", [P, G])
        x1 = per_stream("x1", [P, G, P])
        x2 = per_stream("x2", [P, G, P])
        x3 = per_stream("x3", [P, G, P])
        x4 = per_stream("x4", [P, G, P])
        hT = per_stream("hT", [P, W])
        h_n = per_stream("h_n", [P, G, P])
        agg = per_stream("agg", [P, W])
        t_r = per_stream("t_r", [P, W])
        t_z = per_stream("t_z", [P, W])
        h_half = per_stream("h_half", [P, W])
        pre = per_stream("pre", [P, W])
        cand = per_stream("cand", [P, W])
        diff = per_stream("diff", [P, W])
        h2 = per_stream("h2", [P, G, P])
        hid = per_stream("hid", [P, 2, W])
        x_of_ln = [x1, x2, x3, x4]

        s_const = ctx.enter_context(nc.semaphore("const_loaded"))
        s_pool0 = ctx.enter_context(nc.semaphore("pool_setup"))
        s_dve0 = ctx.enter_context(nc.semaphore("dve_setup"))
        s_pe0 = ctx.enter_context(nc.semaphore("pe_setup"))
        s_start = ctx.enter_context(nc.semaphore("setup_done"))
        x_loaded = [signal(f"x_loaded{s}", 1, 16) for s in range(S)]
        adj_loaded = [signal(f"adj_loaded{s}", 1, 16) for s in range(S)]
        stored = [signal(f"stored{s}", 1, 16) for s in range(S)]

        adjT_ps, adjT_sb = signal("adjT_ps", S), signal("adjT_sb", S)
        xT_ps, xT_sb = signal("xT_ps", S), signal("xT_sb", S)
        q_ps, q_sb = signal("q_ps", 2 * S), signal("q_sb", 2 * S)
        k_ps, k_sb = signal("k_ps", 2 * S), signal("k_sb", 2 * S)
        v_ps, v_sb = signal("v_ps", S), signal("v_sb", S)
        adj_on_sb = signal("adj_on_sb", S)
        off_sb, deg_sb, dis_sb = signal("off_sb", S), signal("deg_sb", S), signal("dis_sb", S)
        res_sb = signal("res_sb", 2 * S)
        adj2_sb, adj3_sb = signal("adj2_sb", S), signal("adj3_sb", S)
        s_ps, max_sb = signal("s_ps", units), signal("max_sb", units)
        rows_ps = signal("rows_ps", 4 * units)
        m_ps, shifted = signal("m_ps", units), signal("shifted", units)
        st_ps, exp_sb, prob_sb = signal("st_ps", units), signal("exp_sb", units), signal("prob_sb", units)
        o_ps, rsum_sb, norm_sb = signal("o_ps", units), signal("rsum_sb", units), signal("norm_sb", units)
        oT_ps, oT_sb, y_ps = signal("oT_ps", S), signal("oT_sb", S), signal("y_ps", S)
        t_sb = signal("t_sb", 4 * S)
        stats_sb = signal("stats_sb", 4 * S)
        var_sb = signal("var_sb", 4 * S)
        vareps_sb = signal("vareps_sb", 4 * S)
        rstd_sb = signal("rstd_sb", 4 * S)
        ln_sb = signal("ln_sb", 4 * S)
        h0_ps = signal("h0_ps", S)
        h_sb = signal("h_sb", (layers + 1) * S)
        hn_ps, hn_sb = signal("hn_ps", layers * S), signal("hn_sb", (layers - 1) * S)
        agg_ps, agg_sb = signal("agg_ps", layers * S), signal("agg_sb", layers * S)
        r_ps, z_ps = signal("r_ps", layers * S), signal("z_ps", layers * S)
        hh_ps, i_ps = signal("hh_ps", layers * S), signal("i_ps", layers * S)
        r_sb, z_sb = signal("r_sb", layers * S), signal("z_sb", layers * S)
        half_sb, gated_sb = signal("half_sb", layers * S), signal("gated_sb", layers * S)
        pre_sb, cand_sb = signal("pre_sb", layers * S), signal("cand_sb", layers * S)
        diff_sb, zdiff_sb = signal("diff_sb", layers * S), signal("zdiff_sb", layers * S)
        x2T_ps, x2T_sb = signal("x2T_ps", S), signal("x2T_sb", S)
        h2_ps, h2_sb, d2_ps = signal("h2_ps", S), signal("h2_sb", S), signal("d2_ps", S)
        hs_ps, hs_sb = signal("hs_ps", S), signal("hs_sb", S)
        hid_ps, hid_sb, y3_ps = signal("hid_ps", 2 * S), signal("hid_sb", 2 * S), signal("y3_ps", S)

        x_dram = t["x"].rearrange("b n d -> n b d")
        adj_dram = t["adj"].rearrange("b n m -> n b m")
        out_dram = out.rearrange("b n d -> n b d")

        loads = [
            (wv[:], t["L0_Wv_T"]), (wo[:], t["L0_Wo_T"]),
            (w_l[:], t["L1_weight_T"].rearrange("l e d -> e l d")),
            (w_ih[:], t["L1_w_ih_T"]), (w_hh[:], t["L1_w_hh_T"]),
            (b_ih[:], t["L1_b_ih"]), (b_hh[:], t["L1_b_hh"]),
            (w2g[:], t["L2_W_T"]), (w31[:], t["L3_W1"]), (b31[:], t["L3_b1"]),
            (w32[:], t["L3_W2"].rearrange("(c p) o -> p c o", p=P)),
            (nodemask[:], t["nodemask_T"]),
            (bo[:], t["L0_bo"].to_broadcast([P, P])), (b2g[:], t["L2_b"].to_broadcast([P, P])),
            (b32[:], t["L3_b2"].to_broadcast([P, P])), (eps3[:], t["L3_eps"].to_broadcast([P, 1])),
        ]
        padded = [(wq, t["L0_Wq_T"]), (wk, t["L0_Wk_T"])]
        n_const = len(loads) + 2 * len(padded)

        block = ctx.enter_context(nc.Block())

        @block.sync
        def _(sp):
            for s in signals:
                sp.sem_inc(s.sem, s.per_round * s.unit)
            for dst, src in loads:
                sp.dma_start(dst, src).then_inc(s_const, 16)
            sp.wait_ge(s_pool0, 4)
            for dst, src in padded:
                for h in range(2):
                    sp.dma_start(dst[:, h, :, 0:dh],
                                 src[:, h * (P // 2):(h + 1) * (P // 2)].rearrange("p (h d) -> p h d", d=dh)
                                 ).then_inc(s_const, 16)
            with sp.Fori(0, rounds) as rnd:
                for s in range(S):
                    first = sp.snap(rnd * (G * S) + s * G)
                    of_pair = sp.snap(adjT_ps.after(rnd, s + 1 - S))
                    of_res = sp.snap(res_sb.after(rnd, s + 1 - 2 * S))
                    sp.wait_ge(adjT_ps.sem, of_pair)
                    sp.wait_ge(adj_on_sb.sem, of_pair)
                    sp.wait_ge(off_sb.sem, of_pair)
                    sp.dma_start(adj[s][:], adj_dram[:, bass.ds(first, G), :]).then_inc(adj_loaded[s].sem, 16)
                    sp.wait_ge(s_pool0, 1)
                    sp.wait_ge(xT_ps.sem, of_pair)
                    sp.wait_ge(res_sb.sem, of_res)
                    sp.dma_start(x_in[s][:], x_dram[:, bass.ds(first, G), :]).then_inc(x_loaded[s].sem, 16)

        @block.gpsimd
        def _(pool):
            pool.memset(ident[:], 0.0).then_inc(s_pool0, 1)
            pool.memset(off_diag[:], 1.0).then_inc(s_pool0, 1)
            pool.memset(wq[:], 0.0).then_inc(s_pool0, 1)
            pool.memset(wk[:], 0.0).then_inc(s_pool0, 1)
            pool.memset(power[:], -0.5).then_inc(s_pool0, 1)
            pool.memset(k_bias[:], 0.0).then_inc(s_pool0, 1)
            pool.memset(ln_eps[:], LN_EPS).then_inc(s_pool0, 1)
            for s in range(S):
                pool.memset(maxima[s][:], 0.0).then_inc(s_pool0, 1)
                pool.memset(v1[s][:], 1.0).then_inc(s_pool0, 1)
            pool.wait_ge(s_pool0, 7 + 2 * S)
            pool.affine_select(out=ident[:], in_=ident[:], compare_op=ALU.not_equal, fill=1.0, base=0,
                               pattern=[[-1, P]], channel_multiplier=1).then_inc(s_pool0, 1)
            pool.affine_select(out=off_diag[:], in_=off_diag[:], compare_op=ALU.not_equal, fill=0.0, base=0,
                               pattern=[[-1, P]], channel_multiplier=1).then_inc(s_pool0, 1)
            for j in range(half_heads):
                pool.wait_ge(s_pool0, 9 + 2 * S + j)
                pool.affine_select(out=k_bias[:], in_=k_bias[:], compare_op=ALU.not_equal, fill=-1.0,
                                   base=-(pad * j + dh), pattern=[[0, 1]], channel_multiplier=1).then_inc(s_pool0, 1)
            pool.wait_ge(s_start, 1)

            def rsqrt(rnd, n, s, src, dst, wait, done):
                pool.wait_ge(var_sb.sem, wait)
                pool.tensor_tensor(var_eps[s][:], src, ln_eps[:], ALU.add).then_inc(vareps_sb.sem, 1)
                pool.wait_ge(vareps_sb.sem, vareps_sb.after(rnd, n * S + s + 1))
                pool.tensor_tensor(dst, var_eps[s][:], power[:], ALU.pow).then_inc(done.sem, 1)

            def norm(rnd, n):
                for s in range(S):
                    rsqrt(rnd, n, s, mean_var[s][:, :, 1], rstd[s][:],
                          var_sb.after(rnd, n * S + s + 1), rstd_sb)

            with pool.Fori(0, rounds) as rnd:
                for s in range(S):
                    pool.wait_ge(adj_loaded[s].sem, adj_loaded[s].after(rnd, 1))
                    pool.wait_ge(deg_sb.sem, deg_sb.after(rnd, s + 1 - S))
                    pool.tensor_tensor(adj_off[s][:], adj[s][:],
                                       off_diag[:].unsqueeze(1).to_broadcast([P, G, P]),
                                       ALU.mult).then_inc(off_sb.sem, 1)
                    pool.wait_ge(x_loaded[s].sem, x_loaded[s].after(rnd, 1))
                    pool.wait_ge(t_sb.sem, t_sb.after(rnd, s + 1 - S))
                    pool.tensor_tensor(res[s][:], x_in[s][:], bo[:].unsqueeze(1).to_broadcast([P, G, P]),
                                       ALU.add).then_inc(res_sb.sem, 1)
                for s in range(S):
                    pool.wait_ge(deg_sb.sem, deg_sb.after(rnd, s + 1))
                    pool.wait_ge(t_sb.sem, t_sb.after(rnd, 3 * S - 4 * S + s + 1 - S + S))
                    pool.tensor_tensor(dis[s][:], deg[s][:], power[:], ALU.pow).then_inc(dis_sb.sem, 1)
                norm(rnd, 0)
                for s in range(S):
                    pool.wait_ge(dis_sb.sem, dis_sb.after(rnd, s + 1))
                    pool.wait_ge(adjT_sb.sem, adjT_sb.after(rnd, s + 1))
                    pool.wait_ge(hs_ps.sem, hs_ps.after(rnd, s + 1 - S))
                    pool.tensor_tensor(adj2[s][:], adjT[s][:],
                                       dis[s][:].unsqueeze(2).to_broadcast([P, G, P]),
                                       ALU.mult).then_inc(adj2_sb.sem, 1)
                    pool.tensor_tensor(adj3[s][:], adjT[s][:],
                                       eps_ident[:].unsqueeze(1).to_broadcast([P, G, P]),
                                       ALU.add).then_inc(adj3_sb.sem, 1)
                norm(rnd, 1)
                norm(rnd, 2)
                for s in range(S):
                    pool.wait_ge(ln_sb.sem, ln_sb.after(rnd, 2 * S + s + 1))
                    pool.tensor_tensor(res[s][:], x3[s][:], b32[:].unsqueeze(1).to_broadcast([P, G, P]),
                                       ALU.add).then_inc(res_sb.sem, 1)
                norm(rnd, 3)

        @block.scalar
        def _(act):
            act.wait_ge(s_start, 1)
            with act.Fori(0, rounds) as rnd:
                for s in range(S):
                    act.wait_ge(adj3_sb.sem, adj3_sb.after(rnd, s + 1 - S))
                    act.wait_ge(adjT_ps.sem, adjT_ps.after(rnd, s + 1))
                    act.activation(adjT[s][:], bank[s][:], ACT.Identity).then_inc(adjT_sb.sem, 1)
                    act.wait_ge(xT_ps.sem, xT_ps.after(rnd, s + 1))
                    act.activation(xT[s][:], bank[2 + s][:], ACT.Identity).then_inc(xT_sb.sem, 1)
                for s in range(S):
                    for h in range(2):
                        act.wait_ge(k_ps.sem, k_ps.after(rnd, 2 * s + h + 1))
                        act.activation(kT[s][:, h], bank[6 + h][:], ACT.Identity,
                                       bias=k_bias[:]).then_inc(k_sb.sem, 1)
                for u in range(units):
                    act.wait_ge(st_ps.sem, st_ps.after(rnd, u + 1))
                    act.wait_ge(o_ps.sem, o_ps.after(rnd, u - 1))
                    ev = e[u % 2][:].rearrange("p (c m) n -> p m c n", m=2)
                    for b in range(2):
                        ins = act.activation(e[u % 2][:].rearrange("p (c m b) n -> p b m c n", m=2, b=2)[:, b],
                                             ps_st[b][:].rearrange("p (m c n) -> p m c n", m=2, c=2), ACT.Exp)
                    ins.then_inc(exp_sb.sem, 1)
                for s in range(S):
                    act.wait_ge(oT_ps.sem, oT_ps.after(rnd, s + 1))
                    act.activation(oT[s][:], bank[s][:], ACT.Identity).then_inc(oT_sb.sem, 1)
                for s in range(S):
                    act.wait_ge(h0_ps.sem, h0_ps.after(rnd, s + 1))
                    act.activation(hT[s][:], bank[s][:], ACT.Identity).then_inc(h_sb.sem, 1)
                for l in range(layers):
                    for s in range(S):
                        k = l * S + s + 1
                        if l:
                            act.wait_ge(hn_ps.sem, hn_ps.after(rnd, k - S))
                            act.activation(h_n[s][:], bank[s][:], ACT.Identity).then_inc(hn_sb.sem, 1)
                        act.wait_ge(hh_ps.sem, hh_ps.after(rnd, k))
                        act.activation(h_half[s][:], bank[6][:], ACT.Identity, scale=0.5,
                                       bias=b_half[:, 2:3]).then_inc(half_sb.sem, 1)
                        act.wait_ge(r_ps.sem, r_ps.after(rnd, k))
                        act.activation(t_r[s][:], bank[4][:], ACT.Tanh, scale=0.5,
                                       bias=b_half[:, 0:1]).then_inc(r_sb.sem, 1)
                        act.wait_ge(z_ps.sem, z_ps.after(rnd, k))
                        act.activation(t_z[s][:], bank[5][:], ACT.Tanh, scale=0.5,
                                       bias=b_half[:, 1:2]).then_inc(z_sb.sem, 1)
                        act.wait_ge(pre_sb.sem, pre_sb.after(rnd, k))
                        act.activation(cand[s][:], pre[s][:], ACT.Tanh, bias=b_ih[:, 2:3]).then_inc(cand_sb.sem, 1)
                for s in range(S):
                    act.wait_ge(x2T_ps.sem, x2T_ps.after(rnd, s + 1))
                    act.activation(xT[s][:], bank[s][:], ACT.Identity).then_inc(x2T_sb.sem, 1)
                for s in range(S):
                    act.wait_ge(hs_ps.sem, hs_ps.after(rnd, s + 1))
                    act.activation(hT[s][:], bank[s][:], ACT.Identity).then_inc(hs_sb.sem, 1)
                for s in range(S):
                    for h in range(2):
                        act.wait_ge(hid_ps.sem, hid_ps.after(rnd, 2 * s + h + 1))
                        act.activation(hid[s][:, h], bank[4 + 2 * s + h][:], ACT.Relu,
                                       bias=b31[:, h:h + 1]).then_inc(hid_sb.sem, 1)
                for s in range(S):
                    act.wait_ge(ln_sb.sem, ln_sb.after(rnd, 3 * S + s + 1))
                    act.dma_start(out_dram[:, bass.ds(rnd * (G * S) + s * G, G), :],
                                  x4[s][:]).then_inc(stored[s].sem, 16)
            for s in range(S):
                act.wait_ge(stored[s].sem, 16 * (rounds + 1))

        @block.vector
        def _(dve):
            dve.wait_ge(s_const, 16 * n_const)
            dve.tensor_scalar(wq[:], wq[:], float(dh) ** -0.5, None, ALU.mult).then_inc(s_dve0, 1)
            dve.tensor_tensor(b_half[:, 0:2], b_ih[:, 0:2], b_hh[:, 0:2], ALU.add).then_inc(s_dve0, 1)
            dve.tensor_scalar(b_half[:, 2:3], b_hh[:, 2:3], 0.5, None, ALU.mult).then_inc(s_dve0, 1)
            dve.tensor_scalar(eps3[:], eps3[:], 1.0, None, ALU.add).then_inc(s_dve0, 1)
            dve.wait_ge(s_dve0, 4)
            dve.tensor_scalar(b_half[:, 0:2], b_half[:, 0:2], 0.5, None, ALU.mult).then_inc(s_dve0, 1)
            dve.wait_ge(s_pool0, 9 + 2 * S + half_heads)
            dve.tensor_scalar(eps_ident[:], ident[:], eps3[:, 0:1], None, ALU.mult).then_inc(s_dve0, 1)
            for l in range(layers):
                dve.wait_ge(s_pe0, l + 1)
                dve.tensor_copy(w_in[:, l], bank[l % 2][:, 0:3 * P]).then_inc(s_dve0, 1)
            dve.wait_ge(s_dve0, 6 + layers)
            dve.sem_inc(s_start, 1)

            def norm(rnd, n):
                for s in range(S):
                    k = n * S + s + 1
                    dve.wait_ge(t_sb.sem, t_sb.after(rnd, k))
                    for g in range(G):
                        ins = dve.bn_stats(stats[s][:, g], t_ln[s][:, g])
                    ins.then_inc(stats_sb.sem, 1)
                for s in range(S):
                    k = n * S + s + 1
                    dve.wait_ge(s_start, 1)
                    dve.wait_ge(stats_sb.sem, stats_sb.after(rnd, k))
                    for g in range(G):
                        ins = dve.bn_aggr(mean_var[s][:, g], stats[s][:, g])
                    ins.then_inc(var_sb.sem, 1)
                for s in range(S):
                    k = n * S + s + 1
                    dve.wait_ge(rstd_sb.sem, rstd_sb.after(rnd, k))
                    if n == 3:
                        dve.wait_ge(stored[s].sem, stored[s].after(rnd, 0))
                    for g in range(G):
                        ins = dve.tensor_scalar(x_of_ln[n][s][:, g], t_ln[s][:, g], mean_var[s][:, g, 0:1],
                                                rstd[s][:, g:g + 1], ALU.subtract, ALU.mult)
                    ins.then_inc(ln_sb.sem, 1)

            with dve.Fori(0, rounds) as rnd:
                for s in range(S):
                    dve.wait_ge(adj_loaded[s].sem, adj_loaded[s].after(rnd, 1))
                    dve.tensor_scalar(adj_on[s][:], adj[s][:], 0.0, None, ALU.not_equal).then_inc(adj_on_sb.sem, 1)
                for s in range(S):
                    dve.wait_ge(off_sb.sem, off_sb.after(rnd, s + 1))
                    dve.reduce_sum(deg[s][:], adj_off[s][:], AX_X).then_inc(deg_sb.sem, 1)
                for s in range(S):
                    for h in range(2):
                        dve.wait_ge(q_ps.sem, q_ps.after(rnd, 2 * s + h + 1))
                        dve.tensor_copy(qT[s][:, h], bank[4 + h][:]).then_inc(q_sb.sem, 1)
                    dve.wait_ge(v_ps.sem, v_ps.after(rnd, s + 1))
                    dve.tensor_copy(v1[s][:, :, :, 0:dh],
                                    bank[s][:].rearrange("p (g h d) -> p g h d", g=G, d=dh)).then_inc(v_sb.sem, 1)
                for k in range(units + 3):
                    u = k - 2
                    if 0 <= u < units:
                        s, g = divmod(u, G)
                        dve.wait_ge(exp_sb.sem, exp_sb.after(rnd, u + 1))
                        dve.scalar_tensor_tensor(e[u % 2][:], adjT[s][:, g].unsqueeze(1).to_broadcast([P, heads, P]),
                                                 ADJ_EPS, e[u % 2][:], ALU.add, ALU.mult).then_inc(prob_sb.sem, 1)
                    u = k - 1
                    if 0 <= u < units:
                        s, g = divmod(u, G)
                        dve.wait_ge(m_ps.sem, m_ps.after(rnd, u + 1))
                        q = qT[s][:].rearrange("p h (g n) -> p h g n", g=G)[:, :, g]
                        dve.tensor_tensor(q, ps_m[u % 2][:, 0:2 * P].rearrange("p (h n) -> p h n", h=2), q,
                                          ALU.add).then_inc(shifted.sem, 1)
                    u = k
                    if u < units:
                        s, g = divmod(u, G)
                        dve.wait_ge(s_ps.sem, s_ps.after(rnd, u + 1))
                        for b in range(2):
                            ins = dve.tensor_reduce(
                                maxima[s][:, g].rearrange("p c (m b) r -> p b m c r", b=2)[:, b, :, :, dh],
                                ps_s[b][:].rearrange("p (m c n) -> p m c n", m=2, c=2), AX_X, ALU.max)
                        ins.then_inc(max_sb.sem, 1)
                    u = k - 3
                    if 0 <= u < units:
                        s, g = divmod(u, G)
                        o = ps_o[u % 2][:, 0:heads * vw].rearrange("p (h w) -> p h w", w=vw)
                        dve.wait_ge(o_ps.sem, o_ps.after(rnd, u + 1))
                        dve.reciprocal(r_sum[u % 2][:], o[:, :, dh]).then_inc(rsum_sb.sem, 1)
                        dve.wait_ge(rsum_sb.sem, rsum_sb.after(rnd, u + 1))
                        dve.tensor_tensor(o_n[s][:, g], o[:, :, 0:dh],
                                          r_sum[u % 2][:].unsqueeze(2).to_broadcast([P, heads, dh]),
                                          ALU.mult).then_inc(norm_sb.sem, 1)
                for s in range(S):
                    dve.wait_ge(y_ps.sem, y_ps.after(rnd, s + 1))
                    dve.wait_ge(res_sb.sem, res_sb.after(rnd, s + 1))
                    dve.tensor_tensor(t_ln[s][:], bank[6 + s][:].rearrange("p (g n) -> p g n", g=G), res[s][:],
                                      ALU.add).then_inc(t_sb.sem, 1)
                norm(rnd, 0)
                for l in range(layers):
                    for s in range(S):
                        k = l * S + s + 1
                        dve.wait_ge(agg_ps.sem, agg_ps.after(rnd, k))
                        dve.tensor_copy(agg[s][:], bank[2 + s][:]).then_inc(agg_sb.sem, 1)
                        dve.wait_ge(r_sb.sem, r_sb.after(rnd, k))
                        dve.wait_ge(half_sb.sem, half_sb.after(rnd, k))
                        dve.scalar_tensor_tensor(h_half[s][:], t_r[s][:], 1.0, h_half[s][:], ALU.add,
                                                 ALU.mult).then_inc(gated_sb.sem, 1)
                        dve.wait_ge(gated_sb.sem, gated_sb.after(rnd, k))
                        dve.wait_ge(i_ps.sem, i_ps.after(rnd, k))
                        dve.tensor_tensor(pre[s][:], bank[7][:], h_half[s][:], ALU.add).then_inc(pre_sb.sem, 1)
                        dve.wait_ge(h_sb.sem, h_sb.after(rnd, k))
                        dve.wait_ge(cand_sb.sem, cand_sb.after(rnd, k))
                        dve.tensor_tensor(diff[s][:], hT[s][:], cand[s][:], ALU.subtract).then_inc(diff_sb.sem, 1)
                        dve.wait_ge(diff_sb.sem, diff_sb.after(rnd, k))
                        dve.wait_ge(z_sb.sem, z_sb.after(rnd, k))
                        dve.scalar_tensor_tensor(diff[s][:], t_z[s][:], 1.0, diff[s][:], ALU.add,
                                                 ALU.mult).then_inc(zdiff_sb.sem, 1)
                        dve.wait_ge(zdiff_sb.sem, zdiff_sb.after(rnd, k))
                        dve.scalar_tensor_tensor(hT[s][:], diff[s][:], 0.5, cand[s][:], ALU.mult,
                                                 ALU.add).then_inc(h_sb.sem, 1)
                for s in range(S):
                    dve.wait_ge(hn_ps.sem, hn_ps.after(rnd, (layers - 1) * S + s + 1))
                    for g in range(G):
                        ins = dve.scalar_tensor_tensor(
                            t_ln[s][:, g], bank[s][:, g * P:(g + 1) * P],
                            nodemask[:, bass.ds(rnd * (G * S) + s * G + g, 1)], x1[s][:, g], ALU.mult, ALU.add)
                    ins.then_inc(t_sb.sem, 1)
                norm(rnd, 1)
                for s in range(S):
                    dve.wait_ge(h2_ps.sem, h2_ps.after(rnd, s + 1))
                    dve.tensor_tensor(h2[s][:], bank[2 + s][:].rearrange("p (g n) -> p g n", g=G),
                                      b2g[:].unsqueeze(1).to_broadcast([P, G, P]), ALU.add).then_inc(h2_sb.sem, 1)
                for s in range(S):
                    dve.wait_ge(d2_ps.sem, d2_ps.after(rnd, s + 1))
                    for g in range(G):
                        ins = dve.scalar_tensor_tensor(t_ln[s][:, g], bank[4 + s][:, g * P:(g + 1) * P],
                                                       dis[s][:, g:g + 1], x2[s][:, g], ALU.mult, ALU.add)
                    ins.then_inc(t_sb.sem, 1)
                norm(rnd, 2)
                for s in range(S):
                    dve.wait_ge(y3_ps.sem, y3_ps.after(rnd, s + 1))
                    dve.wait_ge(res_sb.sem, res_sb.after(rnd, S + s + 1))
                    dve.tensor_tensor(t_ln[s][:], bank[2 + s][:].rearrange("p (g n) -> p g n", g=G), res[s][:],
                                      ALU.add).then_inc(t_sb.sem, 1)
                norm(rnd, 3)

        @block.tensor
        def _(pe):
            pe.wait_ge(s_const, 16 * n_const)
            for l in range(layers):
                if l >= 2:
                    pe.wait_ge(s_dve0, 6 + l - 1)
                pe.matmul(bank[l % 2][:, 0:3 * P], w_l[:, l], w_ih[:], start=True, stop=True).then_inc(s_pe0, 1)
            pe.wait_ge(s_start, 1)

            def turn(dst, src, done):
                for g in range(G):
                    ins = pe.transpose(dst[:, g * P:(g + 1) * P], src[:, g * P:(g + 1) * P], ident[:])
                ins.then_inc(done.sem, 1)

            def flat(a):
                return a[:].rearrange("p g n -> p (g n)")

            def per_graph(dst, lhs, rhs, done):
                for g in range(G):
                    ins = pe.matmul(dst[:, g * P:(g + 1) * P], lhs(g), rhs(g), start=True, stop=True)
                ins.then_inc(done.sem, 1)

            def blk(a):
                return lambda g: a[:, g * P:(g + 1) * P]

            def row(a):
                return lambda g: a[:, g]

            with pe.Fori(0, rounds) as rnd:
                for s in range(S):
                    pe.wait_ge(adj_loaded[s].sem, adj_loaded[s].after(rnd, 1))
                    turn(bank[s], flat(adj[s]), adjT_ps)
                    pe.wait_ge(x_loaded[s].sem, x_loaded[s].after(rnd, 1))
                    pe.wait_ge(t_sb.sem, t_sb.after(rnd, s + 1 - S))
                    turn(bank[2 + s], flat(x_in[s]), xT_ps)
                for s in range(S):
                    pe.wait_ge(xT_sb.sem, xT_sb.after(rnd, s + 1))
                    for h in range(2):
                        pe.wait_ge(q_sb.sem, q_sb.after(rnd, 2 * s + h + 1 - 2))
                        pe.matmul(bank[4 + h][:], wq[:, h].rearrange("p h d -> p (h d)"), xT[s][:],
                                  start=True, stop=True).then_inc(q_ps.sem, 1)
                        pe.wait_ge(k_sb.sem, k_sb.after(rnd, 2 * s + h + 1 - 2))
                        pe.matmul(bank[6 + h][:], wk[:, h].rearrange("p h d -> p (h d)"), xT[s][:],
                                  start=True, stop=True).then_inc(k_ps.sem, 1)
                    pe.wait_ge(adjT_sb.sem, adjT_sb.after(rnd, s + 1))
                    per_graph(bank[s], blk(xT[s]), lambda g: wv[:], v_ps)

                def head_products(dst, lhs, rhs, s, g, done, call):
                    for j in range(half_heads):
                        if j >= 2:
                            pe.wait_ge(rows_ps.sem, rows_ps.after(rnd, 2 * call + j - 1))
                        for c in range(2):
                            rows = slice(pad * j, pad * (j + 1))
                            cols = slice(((j // 2) * 2 + c) * P, ((j // 2) * 2 + c + 1) * P)
                            ins = pe.matmul(dst[j % 2][:, cols], lhs[s][rows, c, g * P:(g + 1) * P],
                                            rhs[s][rows, c, g * P:(g + 1) * P], start=True, stop=True)
                        if j < 2:
                            ins.then_inc(rows_ps.sem, 1)
                    ins.then_inc(done.sem, 1)

                calls = [c for k in range(units + 1) for c in (("s", k), ("st", k - 1)) if 0 <= c[1] < units]
                for k in range(units + 2):
                    u = k
                    if u < units:
                        s, g = divmod(u, G)
                        if u == 0:
                            pe.wait_ge(q_sb.sem, q_sb.after(rnd, 2 * S))
                            pe.wait_ge(k_sb.sem, k_sb.after(rnd, 2 * S))
                            pe.wait_ge(v_sb.sem, v_sb.after(rnd, S))
                        pe.wait_ge(max_sb.sem, max_sb.after(rnd, u))
                        head_products(ps_s, qT, kT, s, g, s_ps, calls.index(('s', u)))
                    u = k - 1
                    if 0 <= u < units:
                        s, g = divmod(u, G)
                        pe.wait_ge(max_sb.sem, max_sb.after(rnd, u + 1))
                        pe.wait_ge(shifted.sem, shifted.after(rnd, u - 1))
                        for c in range(2):
                            ins = pe.transpose(ps_m[u % 2][:, c * P:(c + 1) * P],
                                               maxima[s][:, g, c].rearrange("p h r -> p (h r)"), ident[:])
                        ins.then_inc(m_ps.sem, 1)
                    u = k - 2
                    if 0 <= u < units:
                        s, g = divmod(u, G)
                        pe.wait_ge(prob_sb.sem, prob_sb.after(rnd, u + 1))
                        pe.wait_ge(norm_sb.sem, norm_sb.after(rnd, u - 1))
                        for h in range(heads):
                            ins = pe.matmul(ps_o[u % 2][:, h * vw:(h + 1) * vw], e[u % 2][:, h], v1[s][:, g, h],
                                            start=True, stop=True)
                        ins.then_inc(o_ps.sem, 1)
                    u = k - 1
                    if 0 <= u < units:
                        s, g = divmod(u, G)
                        pe.wait_ge(shifted.sem, shifted.after(rnd, u + 1))
                        pe.wait_ge(exp_sb.sem, exp_sb.after(rnd, u))
                        head_products(ps_st, kT, qT, s, g, st_ps, calls.index(('st', u)))
                for s in range(S):
                    pe.wait_ge(norm_sb.sem, norm_sb.after(rnd, (s + 1) * G))
                    turn(bank[s], o_n[s][:].rearrange("p g h d -> p (g h d)"), oT_ps)
                for s in range(S):
                    pe.wait_ge(oT_sb.sem, oT_sb.after(rnd, s + 1))
                    per_graph(bank[6 + s], blk(oT[s]), lambda g: wo[:], y_ps)
                for s in range(S):
                    pe.wait_ge(ln_sb.sem, ln_sb.after(rnd, s + 1))
                    turn(bank[s], flat(x1[s]), h0_ps)
                for l in range(layers):
                    for s in range(S):
                        k = l * S + s + 1
                        pe.wait_ge(h_sb.sem, h_sb.after(rnd, k))
                        if l:
                            turn(bank[s], hT[s], hn_ps)
                        hidden = [(bank[4], 0, r_sb), (bank[5], 1, z_sb), (bank[6], 2, half_sb)]
                        for b, gate, read in hidden:
                            pe.wait_ge(read.sem, read.after(rnd, k - 1))
                            ins = pe.matmul(b[:], w_hh[:, gate * P:(gate + 1) * P], hT[s][:],
                                            start=True, stop=(gate == 2))
                        ins.then_inc(hh_ps.sem, 1)
                        if l:
                            pe.wait_ge(hn_sb.sem, hn_sb.after(rnd, k - S))
                        h_rows = h_n if l else x1
                        per_graph(bank[2 + s], row(h_rows[s]), row(adj_on[s]), agg_ps)
                        pe.wait_ge(agg_sb.sem, agg_sb.after(rnd, k))
                        for b, gate, done in ((bank[4], 0, r_ps), (bank[5], 1, z_ps)):
                            pe.matmul(b[:], w_in[:, l, gate * P:(gate + 1) * P], agg[s][:],
                                      start=False, stop=True).then_inc(done.sem, 1)
                        pe.wait_ge(pre_sb.sem, pre_sb.after(rnd, k - 1))
                        pe.matmul(bank[7][:], w_in[:, l, 2 * P:3 * P], agg[s][:],
                                  start=True, stop=True).then_inc(i_ps.sem, 1)
                for s in range(S):
                    pe.wait_ge(h_sb.sem, h_sb.after(rnd, layers * S + s + 1))
                    turn(bank[s], hT[s], hn_ps)
                for s in range(S):
                    pe.wait_ge(ln_sb.sem, ln_sb.after(rnd, S + s + 1))
                    turn(bank[s], flat(x2[s]), x2T_ps)
                for s in range(S):
                    pe.wait_ge(x2T_sb.sem, x2T_sb.after(rnd, s + 1))
                    per_graph(bank[2 + s], blk(xT[s]), lambda g: w2g[:], h2_ps)
                for s in range(S):
                    pe.wait_ge(h2_sb.sem, h2_sb.after(rnd, s + 1))
                    pe.wait_ge(adj2_sb.sem, adj2_sb.after(rnd, s + 1))
                    per_graph(bank[4 + s], row(adj2[s]), row(h2[s]), d2_ps)
                for s in range(S):
                    pe.wait_ge(ln_sb.sem, ln_sb.after(rnd, 2 * S + s + 1))
                    pe.wait_ge(adj3_sb.sem, adj3_sb.after(rnd, s + 1))
                    per_graph(bank[s], row(x3[s]), row(adj3[s]), hs_ps)
                for s in range(S):
                    pe.wait_ge(hs_sb.sem, hs_sb.after(rnd, s + 1))
                    for h in range(2):
                        pe.matmul(bank[4 + 2 * s + h][:], w31[:, h * P:(h + 1) * P], hT[s][:],
                                  start=True, stop=True).then_inc(hid_ps.sem, 1)
                for s in range(S):
                    pe.wait_ge(hid_sb.sem, hid_sb.after(rnd, 2 * s + 2))
                    for g in range(G):
                        for h in range(2):
                            ins = pe.matmul(bank[2 + s][:, g * P:(g + 1) * P], hid[s][:, h, g * P:(g + 1) * P],
                                            w32[:, h], start=(h == 0), stop=(h == 1))
                    ins.then_inc(y3_ps.sem, 1)


def kernel(**inputs):
    import numpy as np
    import concourse.bacc as bacc
    from concourse.bass_utils import run_bass_kernel_spmd

    a = {n: np.asarray(v) for n, v in inputs.items()}
    lay = {
        "x": a["x"], "adj": a["adj"], "nodemask_T": a["nodemask"].T,
        "L0_Wq_T": a["L0_gnn_Wq"].T, "L0_Wk_T": a["L0_gnn_Wk"].T, "L0_Wv_T": a["L0_gnn_Wv"].T,
        "L0_Wo_T": a["L0_gnn_Wo"].T, "L0_bo": a["L0_gnn_bo"].reshape(1, -1),
        "L1_weight_T": a["L1_gnn_weight"].transpose(0, 2, 1),
        "L1_w_ih_T": a["L1_gnn_w_ih"].T, "L1_w_hh_T": a["L1_gnn_w_hh"].T,
        "L1_b_ih": a["L1_gnn_b_ih"].reshape(3, -1).T, "L1_b_hh": a["L1_gnn_b_hh"].reshape(3, -1).T,
        "L2_W_T": a["L2_gnn_W"].T, "L2_b": a["L2_gnn_b"].reshape(1, -1),
        "L3_eps": a["L3_gnn_eps"].reshape(1, 1), "L3_W1": a["L3_gnn_W1"],
        "L3_b1": a["L3_gnn_b1"].reshape(2, -1).T, "L3_W2": a["L3_gnn_W2"],
        "L3_b2": a["L3_gnn_b2"].reshape(1, -1),
    }
    nc = bacc.Bacc("TRN2", target_bir_lowering=False, num_devices=1)
    arrays, aps = {}, {}
    for name, v in lay.items():
        v = np.ascontiguousarray(v)
        arrays[f"in_{name}"] = v
        aps[name] = nc.dram_tensor(f"in_{name}", v.shape, mybir.dt.from_np(v.dtype), kind="ExternalInput").ap()
    out = nc.dram_tensor("out", a["x"].shape, F32, kind="ExternalOutput").ap()
    gnn_stack(nc, aps, out)
    r = run_bass_kernel_spmd(nc, [arrays], core_ids=[0])
    return r.results[0]["out"]
```

```python
from contextlib import ExitStack

import concourse.bass as bass
from concourse import mybir

F32 = mybir.dt.float32
BF16 = mybir.dt.bfloat16
F16 = mybir.dt.float16
I32 = mybir.dt.int32
ALU = mybir.AluOpType
ACT = mybir.ActivationFunctionType
AX_X = mybir.AxisListType.X
RMAX = bass.bass_isa.ReduceOp.max

P = 128
G = 4
W = G * P
CHAINS = 2
CG = G // CHAINS
CW = CG * P
LANES = 2
LN_EPS = 1e-5
ADJ_EPS = 1e-6

H_SCALE = 2.0 ** 11
AGG_SCALE = 2.0 ** 5
W_TOP = 2.0 ** 8

TERMS = [(0, 0), (0, 1), (0, 2), (1, 0), (1, 1), (2, 0)]
NT = len(TERMS)


class Group:

    def __init__(self, rnd, a, b):
        self.rnd, self.a, self.b = rnd, a, b

    def plus(self, n):
        return Group(self.rnd, self.a, self.b + n)

    def times(self, m, plus):
        c = self.b * m + plus
        return self.rnd * (self.a * m) + c if self.a else c


class Signal:

    AHEAD = 2

    def __init__(self, sem, per_group=1, unit=1):
        self.sem, self.per_group, self.unit = sem, per_group, unit

    def after(self, group, k=1):
        step = self.per_group * self.unit
        return group.times(step, self.AHEAD * step + k * self.unit)


def gnn_stack(nc, t, out):
    B, N, D = t["x"].shape
    assert N == P and D == P
    heads = 8
    dh = D // heads
    hc = heads // 2
    layers = t["L1_weight_T"].shape[0]
    groups = B // G
    vw = dh + 1
    KS = NT * dh
    assert groups % 2 == 0 and CHAINS * layers == 10

    with ExitStack() as ctx:
        def sb(name, shape, dt=F32):
            return ctx.enter_context(nc.sbuf_tensor(name, shape, dt))

        def signal(name, per_group=1, unit=1):
            s = Signal(ctx.enter_context(nc.semaphore(name)), per_group, unit)
            signals.append(s)
            return s

        signals = []
        bank = [ctx.enter_context(nc.psum_tensor(f"bank{i}", [P, W], F32)) for i in range(8)]
        rz, hi, ps_t = bank[0:2], bank[2:4], bank[4]
        ring = bank[5:]
        ps_t16 = ps_t[:].bitcast(F16)

        ident = sb("ident", [P, P])
        ident16 = sb("ident16", [P, P], F16)
        off_diag = sb("off_diag", [P, P])
        eps_ident = sb("eps_ident", [P, P])
        wq = sb("wq", [P, P])
        wk = sb("wk", [P, P])
        wv = sb("wv", [P, P])
        wo = sb("wo", [P, P])
        bo = sb("bo", [P, P])
        w_l = sb("w_l", [P, layers, P])
        w_ih = sb("w_ih", [P, 3 * P])
        w_hh = sb("w_hh", [P, 3 * P])
        w_in = sb("w_in", [P, layers, 3 * P])
        w_hh16 = sb("w_hh16", [P, 2, 3 * P], F16)
        w_in16 = sb("w_in16", [P, 2, layers, 3 * P], F16)
        extremes = sb("extremes", [P, 4])
        w_max = sb("w_max", [P, 1])
        w_pow = sb("w_pow", [P, 1])
        w_rec = sb("w_rec", [P, 1])
        s_hh = sb("s_hh", [P, 1])
        s_in = sb("s_in", [P, 1])
        unscale = sb("unscale", [P, 1])
        half_unscale = sb("half_unscale", [P, 1])
        b_ih = sb("b_ih", [P, 3])
        b_hh = sb("b_hh", [P, 3])
        b_half = sb("b_half", [P, 3])
        w2g = sb("w2g", [P, P])
        b2g = sb("b2g", [P, P])
        w31 = sb("w31", [P, 2 * P])
        b31 = sb("b31", [P, 2])
        w32 = sb("w32", [P, 2, P])
        b32 = sb("b32", [P, P])
        eps3 = sb("eps3", [P, 1])
        nodemask = sb("nodemask", [P, B])
        power = sb("power", [P, G])
        ln_eps = sb("ln_eps", [P, G])

        def lanes(name, shape, dt=F32):
            return [sb(f"{name}{i}", shape, dt) for i in range(LANES)]

        x_in = sb("x_in", [P, G, P])
        adj = sb("adj", [P, G, P])
        adj_off = sb("adj_off", [P, G, P])
        adjT = lanes("adjT", [P, G, P])
        adj_on = lanes("adj_on", [P, G, P], F16)
        deg = sb("deg", [P, G])
        dis = lanes("dis", [P, G])
        xT = sb("xT", [P, W])
        parts = [sb(f"{n}_parts", [P, NT, W], BF16) for n in "qk"]
        rest = [sb(f"{n}_rest", [P, W]) for n in "qk"]
        stack = [sb(f"{n}_stack", [P, LANES, heads, W], BF16) for n in "qk"]
        v1 = lanes("v1", [P, G, heads, vw])
        maxima = sb("maxima", [P, heads, G])
        m_parts = sb("m_parts", [heads * G, 3, P], BF16)
        m_rest = sb("m_rest", [heads * G, P])
        e = [sb(f"e{i}", [P, heads, P]) for i in range(2)]
        r_sum = [sb(f"r_sum{i}", [P, heads]) for i in range(2)]
        o_n = sb("o_n", [P, G, heads, dh])
        oT = sb("oT", [P, W])
        res0 = lanes("res0", [P, G, P])
        t_ln = [sb(f"t_ln{i}", [P, G, P]) for i in range(2)]
        stats = [sb(f"stats{i}", [P, G, 6]) for i in range(2)]
        mean_var = [sb(f"mean_var{i}", [P, G, 2]) for i in range(2)]
        var_eps = [sb(f"var_eps{i}", [P, G]) for i in range(2)]
        rstd = [sb(f"rstd{i}", [P, G]) for i in range(2)]
        x1 = lanes("x1", [P, G, P])
        hT = lanes("hT", [P, W])
        h16 = sb("h16", [P, 2, W], F16)
        hn16 = sb("hn16", [P, 2, G, P], F16)
        agg16 = sb("agg16", [P, 2, W], F16)
        t_r = sb("t_r", [P, W])
        t_z = sb("t_z", [P, W])
        h_half = sb("h_half", [P, W])
        pre = sb("pre", [P, W])
        cand = sb("cand", [P, W])
        diff = sb("diff", [P, W])
        adj2 = lanes("adj2", [P, G, P])
        adj3 = lanes("adj3", [P, G, P])
        x2 = sb("x2", [P, G, P])
        x2T = sb("x2T", [P, W])
        h2 = sb("h2", [P, G, P])
        x3 = sb("x3", [P, G, P])
        hsT = sb("hsT", [P, W])
        hid = sb("hid", [P, 2, W])
        res3 = sb("res3", [P, G, P])
        x4 = sb("x4", [P, G, P])

        s_const = ctx.enter_context(nc.semaphore("const_loaded"))
        s_pool0 = ctx.enter_context(nc.semaphore("pool_setup"))
        s_dve0 = ctx.enter_context(nc.semaphore("dve_setup"))
        s_pe0 = ctx.enter_context(nc.semaphore("pe_setup"))
        s_start = ctx.enter_context(nc.semaphore("setup_done"))
        x_loaded = signal("x_loaded", 1, 16)
        adj_loaded = signal("adj_loaded", 1, 16)
        stacked = [signal(f"stacked{c}", heads, 16) for c in range(2)]
        m_stacked = signal("m_stacked", 3, 16)
        stored = signal("stored", 1, 16)
        adjT_ps, adjT_sb = signal("adjT_ps"), signal("adjT_sb")
        xT_ps, xT_sb = signal("xT_ps"), signal("xT_sb")
        qk_ps = [signal("q_ps"), signal("k_ps")]
        part1 = [signal("q_part1"), signal("k_part1")]
        rest1 = [signal("q_rest1"), signal("k_rest1")]
        part2 = [signal("q_part2"), signal("k_part2")]
        part3 = [signal("q_part3"), signal("k_part3")]
        copies = [signal("q_copies"), signal("k_copies")]
        v_ps, v_sb = signal("v_ps"), signal("v_sb")
        adj_on_sb = signal("adj_on_sb")
        off_sb, deg_sb, dis_sb = signal("off_sb"), signal("deg_sb"), signal("dis_sb")
        res0_sb, res3_sb = signal("res0_sb"), signal("res3_sb")
        adj2_sb, adj3_sb = signal("adj2_sb"), signal("adj3_sb")
        s_ps, max_sb = signal("s_ps", 2 * G), signal("max_sb", 2 * G)
        m_ps, m1_sb, mr_sb, m2_sb, m3_sb = (signal(n) for n in ("m_ps", "m1_sb", "mr_sb", "m2_sb", "m3_sb"))
        st_ps, exp_sb, prob_sb = signal("st_ps", 2 * G), signal("exp_sb", 2 * G), signal("prob_sb", 2 * G)
        o_ps, rsum_sb, norm_sb = signal("o_ps", G), signal("rsum_sb", G), signal("norm_sb", G)
        oT_ps, oT_sb, y_ps = signal("oT_ps"), signal("oT_sb"), signal("y_ps")
        t_sb = [signal(f"t_sb{n}") for n in range(4)]
        stats_sb = [signal(f"stats_sb{n}") for n in range(4)]
        var_sb = [signal(f"var_sb{n}") for n in range(4)]
        vareps_sb = [signal(f"vareps_sb{n}") for n in range(4)]
        rstd_sb = [signal(f"rstd_sb{n}") for n in range(4)]
        ln_sb = [signal(f"ln_sb{n}") for n in range(4)]
        h0_ps, h0_sb = signal("h0_ps"), signal("h0_sb")
        steps = CHAINS * layers
        h_sb = signal("h_sb", steps)
        hhi_sb, hlo_sb = signal("hhi_sb", steps), signal("hlo_sb", steps)
        nhi_sb, nlo_sb = signal("nhi_sb", CHAINS), signal("nlo_sb", CHAINS)
        hn_ps, hn_sb = signal("hn_ps", steps - CHAINS), signal("hn_sb", steps - CHAINS)
        agg_ps, agghi_sb, agglo_sb = (signal(n, steps) for n in ("agg_ps", "agghi_sb", "agglo_sb"))
        hh_ps, rz_ps, i_ps = (signal(n, steps) for n in ("hh_ps", "rz_ps", "i_ps"))
        half_sb, r_sb, z_sb = (signal(n, steps) for n in ("half_sb", "r_sb", "z_sb"))
        gated_sb, pre_sb, cand_sb = (signal(n, steps) for n in ("gated_sb", "pre_sb", "cand_sb"))
        diff_sb, zdiff_sb = (signal(n, steps) for n in ("diff_sb", "zdiff_sb"))
        hT_ps = signal("hT_ps")
        x2T_ps, x2T_sb = signal("x2T_ps"), signal("x2T_sb")
        h2_ps, h2_sb, d2_ps = signal("h2_ps"), signal("h2_sb"), signal("d2_ps")
        hs_ps, hs_sb = signal("hs_ps"), signal("hs_sb")
        hid_ps, hid_sb, y3_ps = signal("hid_ps", 2), signal("hid_sb", 2), signal("y3_ps")

        x_dram = t["x"].rearrange("b n d -> n b d")
        adj_dram = t["adj"].rearrange("b n m -> n b m")
        out_dram = out.rearrange("b n d -> n b d")

        loads = [
            (wq[:], t["L0_Wq_T"]), (wk[:], t["L0_Wk_T"]),
            (wv[:], t["L0_Wv_T"]), (wo[:], t["L0_Wo_T"]),
            (w_l[:], t["L1_weight_T"].rearrange("l e d -> e l d")),
            (w_ih[:], t["L1_w_ih_T"]), (w_hh[:], t["L1_w_hh_T"]),
            (b_ih[:], t["L1_b_ih"]), (b_hh[:], t["L1_b_hh"]),
            (w2g[:], t["L2_W_T"]), (w31[:], t["L3_W1"]), (b31[:], t["L3_b1"]),
            (w32[:], t["L3_W2"].rearrange("(c p) o -> p c o", p=P)),
            (nodemask[:], t["nodemask_T"]),
            (bo[:], t["L0_bo"].to_broadcast([P, P])), (b2g[:], t["L2_b"].to_broadcast([P, P])),
            (b32[:], t["L3_b2"].to_broadcast([P, P])), (eps3[:], t["L3_eps"].to_broadcast([P, 1])),
        ]

        def score(*ids):
            return [(("s", i), 1, max_sb, i + 1) for i in ids]

        def exped(*ids):
            return [(("st", i), 1, exp_sb, i + 1) for i in ids]

        def summed(g):
            return [(("o", g), 1, norm_sb, g + 1)]

        pieces = (
            [("hT", -1, t_sb[1], 1)] + score(0) + [("xT", 2, xT_sb, 1)] + score(1)
            + score(2) + [(("qk", 0), 2, rest1[0], 1), (("qk", 1), 2, rest1[1], 1)] + score(3)
            + [("x2T", -1, x2T_sb, 1)] + score(4, 5, 6)
            + score(7) + [("h2", -1, h2_sb, 1), ("v", 2, v_sb, 1), ("m", 1, mr_sb, 1)]
            + [("adjT", 1, adjT_sb, 1), ("d2", -1, t_sb[2], 1)] + exped(0, 1)
            + exped(2) + summed(0) + exped(3, 4)
            + summed(1) + exped(5, 6) + [("hs", -1, hs_sb, 1)]
            + summed(2) + exped(7) + [(("hid", 0), -1, hid_sb, 1)] + summed(3)
            + [(("hid", 1), -1, hid_sb, 2), ("oT", 1, oT_sb, 1), ("y", 1, t_sb[0], 1)]
            + [("y3", -1, t_sb[3], 1), ("h0", 1, h0_sb, 1)]
        )

        def step(s):
            l, c = divmod(s, CHAINS)
            return l, c, s + 1, slice(c * CW, (c + 1) * CW)

        def banks_of():
            return {name: ring[n % len(ring)] for n, (name, *_) in enumerate(pieces)}

        def halves(engine, half):
            def fixed(n):
                runs = [0 <= n + off < groups for off in (2, 1, 0, -1)]
                half(Group(None, 0, n), n % LANES, *runs)

            for n in (-2, -1, 0):
                fixed(n)
            with engine.Fori(0, (groups - 4) // 2) as rnd:
                for n in (1, 2):
                    half(Group(rnd, 2, n), n % LANES, True, True, True, True)
            for n in range(groups - 3, groups + 1):
                fixed(n)

        block = ctx.enter_context(nc.Block())

        @block.sync
        def _(sp):
            for s in signals:
                sp.sem_inc(s.sem, s.AHEAD * s.per_group * s.unit)
            for dst, src in loads:
                sp.dma_start(dst, src).then_inc(s_const, 16)

            def load(dst, src, group, done):
                first = sp.snap(group.times(G, 0)) if group.a else group.times(G, 0)
                sp.dma_start(dst[:], src[:, bass.ds(first, G), :]).then_inc(done.sem, 16)

            load(x_in, x_dram, Group(None, 0, 0), x_loaded)

            def half(t, lane, ahead, head, own, tail):
                far, nxt, last, other = t.plus(2), t.plus(1), t.plus(-1), 1 - lane
                if t.a or 0 <= t.b + 3 < groups:
                    sp.wait_ge(s_pool0, 1)
                    sp.wait_ge(xT_ps.sem, xT_ps.after(far))
                    sp.wait_ge(res0_sb.sem, res0_sb.after(far))
                    load(x_in, x_dram, t.plus(3), x_loaded)
                if head:
                    sp.wait_ge(s_pool0, 1)
                    sp.wait_ge(m3_sb.sem, m3_sb.after(nxt))
                    for i in range(3):
                        sp.dma_start(stack[0][KS + i:KS + i + 1, other].rearrange("p h (g n) -> p (h g) n", g=G),
                                     m_parts[:, i, :]).then_inc(m_stacked.sem, 16)
                if ahead:
                    sp.wait_ge(s_pool0, 1)
                    sp.wait_ge(adjT_ps.sem, adjT_ps.after(nxt))
                    sp.wait_ge(adj_on_sb.sem, adj_on_sb.after(nxt))
                    sp.wait_ge(off_sb.sem, off_sb.after(nxt))
                    load(adj, adj_dram, far, adj_loaded)
                    sp.wait_ge(s_pool0, 1)
                    for i in range(2):
                        sp.wait_ge(part3[i].sem, part3[i].after(far))
                        sp.wait_ge(copies[i].sem, copies[i].after(far))
                    sp.wait_ge(s_pool0, 1)
                    sp.wait_ge(oT_ps.sem, oT_ps.after(t))
                    for h in range(heads):
                        for i in range(2):
                            sp.dma_start(stack[i][0:KS, lane, h, :],
                                         parts[i][h * dh:(h + 1) * dh]).then_inc(stacked[h // hc].sem, 16)
                if tail:
                    sp.wait_ge(s_pool0, 1)
                    sp.wait_ge(ln_sb[3].sem, ln_sb[3].after(last))
                    out_at = sp.snap(last.times(G, 0)) if t.a else last.times(G, 0)
                    sp.dma_start(out_dram[:, bass.ds(out_at, G), :], x4[:]).then_inc(stored.sem, 16)

            halves(sp, half)
            sp.wait_ge(stored.sem, 16 * (groups + Signal.AHEAD))

        @block.gpsimd
        def _(pool):
            pool.memset(ident[:], 0.0).then_inc(s_pool0, 1)
            pool.memset(off_diag[:], 1.0).then_inc(s_pool0, 1)
            pool.memset(power[:], -0.5).then_inc(s_pool0, 1)
            pool.memset(ln_eps[:], LN_EPS).then_inc(s_pool0, 1)
            for i in range(LANES):
                pool.memset(v1[i][:], 1.0).then_inc(s_pool0, 1)
            pool.wait_ge(s_pool0, 6)
            pool.memset(stack[1][KS:KS + 3], -1.0).then_inc(s_pool0, 1)
            pool.wait_ge(s_pool0, 7)
            pool.affine_select(out=ident[:], in_=ident[:], compare_op=ALU.not_equal, fill=1.0, base=0,
                               pattern=[[-1, P]], channel_multiplier=1).then_inc(s_pool0, 1)
            pool.affine_select(out=off_diag[:], in_=off_diag[:], compare_op=ALU.not_equal, fill=0.0, base=0,
                               pattern=[[-1, P]], channel_multiplier=1).then_inc(s_pool0, 1)
            pool.wait_ge(s_dve0, 8 + layers)
            pool.partition_all_reduce(w_max[:], w_rec[:], P, RMAX).then_inc(s_pool0, 1)
            pool.wait_ge(s_start, 1)

            def rsqrt(grp, n):
                i = min(n, 1)
                pool.wait_ge(var_sb[n].sem, var_sb[n].after(grp))
                pool.tensor_tensor(var_eps[i][:], mean_var[i][:, :, 1], ln_eps[:], ALU.add).then_inc(vareps_sb[n].sem, 1)
                pool.wait_ge(vareps_sb[n].sem, vareps_sb[n].after(grp))
                pool.tensor_tensor(rstd[i][:], var_eps[i][:], power[:], ALU.pow).then_inc(rstd_sb[n].sem, 1)

            def half(t, lane, ahead, head, own, tail):
                far, nxt, last, other = t.plus(2), t.plus(1), t.plus(-1), 1 - lane
                if tail:
                    rsqrt(last, 1)
                if ahead:
                    pool.wait_ge(x_loaded.sem, x_loaded.after(far))
                    pool.wait_ge(t_sb[0].sem, t_sb[0].after(t))
                    pool.tensor_tensor(res0[lane][:], x_in[:], bo[:].unsqueeze(1).to_broadcast([P, G, P]),
                                       ALU.add).then_inc(res0_sb.sem, 1)
                if head:
                    pool.wait_ge(adj_loaded.sem, adj_loaded.after(nxt))
                    pool.wait_ge(deg_sb.sem, deg_sb.after(t))
                    pool.tensor_tensor(adj_off[:], adj[:], off_diag[:].unsqueeze(1).to_broadcast([P, G, P]),
                                       ALU.mult).then_inc(off_sb.sem, 1)
                if ahead:
                    for i in range(2):
                        pool.wait_ge(part2[i].sem, part2[i].after(far))
                        pool.tensor_tensor(parts[i][:, (5, 2)[i]], rest[i][:], parts[i][:, (3, 1)[i]],
                                           ALU.subtract).then_inc(part3[i].sem, 1)
                if own:
                    pool.wait_ge(dis_sb.sem, dis_sb.after(t))
                    pool.wait_ge(adjT_sb.sem, adjT_sb.after(t))
                    pool.wait_ge(hs_ps.sem, hs_ps.after(t.plus(-2)))
                    pool.tensor_tensor(adj2[lane][:], adjT[lane][:],
                                       dis[lane][:].unsqueeze(2).to_broadcast([P, G, P]),
                                       ALU.mult).then_inc(adj2_sb.sem, 1)
                    pool.tensor_tensor(adj3[lane][:], adjT[lane][:],
                                       eps_ident[:].unsqueeze(1).to_broadcast([P, G, P]),
                                       ALU.add).then_inc(adj3_sb.sem, 1)
                if tail:
                    rsqrt(last, 2)
                if head:
                    pool.wait_ge(deg_sb.sem, deg_sb.after(nxt))
                    pool.wait_ge(t_sb[2].sem, t_sb[2].after(last))
                    pool.tensor_tensor(dis[other][:], deg[:], power[:], ALU.pow).then_inc(dis_sb.sem, 1)
                if tail:
                    pool.wait_ge(ln_sb[2].sem, ln_sb[2].after(last))
                    pool.wait_ge(t_sb[3].sem, t_sb[3].after(last.plus(-1)))
                    pool.tensor_tensor(res3[:], x3[:], b32[:].unsqueeze(1).to_broadcast([P, G, P]),
                                       ALU.add).then_inc(res3_sb.sem, 1)
                if head:
                    rsqrt(nxt, 0)
                if tail:
                    rsqrt(last, 3)

            halves(pool, half)

        @block.scalar
        def _(act):
            act.wait_ge(s_start, 1)

            def copy_out(dst, src, ready, grp, done, k=1, bias=0.0, func=ACT.Identity):
                act.wait_ge(ready.sem, ready.after(grp, k))
                act.activation(dst, src, func, bias=bias).then_inc(done.sem, 1)

            def half(t, lane, ahead, head, own, tail):
                far, nxt, last, other = t.plus(2), t.plus(1), t.plus(-1), 1 - lane
                slot = banks_of()

                def exps(ids):
                    for i in ids if head else ():
                        c, g = i % 2, i // 2
                        if c == 0:
                            act.wait_ge(o_ps.sem, o_ps.after(nxt, g - 1))
                        act.wait_ge(st_ps.sem, st_ps.after(nxt, i + 1))
                        act.activation(e[g % 2][:, c * hc:(c + 1) * hc],
                                       slot["st", i][:].rearrange("p (h n) -> p h n", h=hc),
                                       ACT.Exp).then_inc(exp_sb.sem, 1)

                def turned(s):
                    l, c, k, cols = step(s)
                    if l:
                        act.wait_ge(hn_ps.sem, hn_ps.after(t, k - CHAINS))
                        act.wait_ge(agg_ps.sem, agg_ps.after(t, k - CHAINS))
                        act.activation(hn16[:, :, c * CG:(c + 1) * CG], ps_t16[:, 0:2 * CW].rearrange(
                            "p (a g n) -> p a g n", a=2, g=CG), ACT.Copy).then_inc(hn_sb.sem, 1)

                def candidate(s):
                    l, c, k, cols = step(s)
                    act.wait_ge(pre_sb.sem, pre_sb.after(t, k))
                    act.wait_ge(h_sb.sem, h_sb.after(t, k - CHAINS))
                    act.activation(cand[:, cols], pre[:, cols], ACT.Tanh, bias=b_ih[:, 2:3]).then_inc(cand_sb.sem, 1)

                def hidden_half(s):
                    l, c, k, cols = step(s)
                    act.wait_ge(hh_ps.sem, hh_ps.after(t, k))
                    act.wait_ge(pre_sb.sem, pre_sb.after(t, k - CHAINS))
                    act.activation(h_half[:, cols], hi[c][:, 0:CW], ACT.Identity, scale=half_unscale[:],
                                   bias=b_half[:, 2:3]).then_inc(half_sb.sem, 1)

                def sums_high(s):
                    l, c, k, cols = step(s)
                    act.wait_ge(agg_ps.sem, agg_ps.after(t, k))
                    act.wait_ge(i_ps.sem, i_ps.after(t, k - CHAINS))
                    act.activation(agg16[:, 0, cols], ps_t[:, 0:CW], ACT.Copy,
                                   scale=AGG_SCALE / H_SCALE).then_inc(agghi_sb.sem, 1)

                def begin(s):
                    if own:
                        turned(s)
                        if s:
                            candidate(s - 1)
                        hidden_half(s)
                        sums_high(s)

                def gates(s):
                    l, c, k, cols = step(s)
                    if own:
                        act.wait_ge(rz_ps.sem, rz_ps.after(t, k))
                        act.wait_ge(zdiff_sb.sem, zdiff_sb.after(t, k - CHAINS))
                        act.activation(t_r[:, cols], rz[c][:, 0:CW], ACT.Tanh, scale=half_unscale[:],
                                       bias=b_half[:, 0:1]).then_inc(r_sb.sem, 1)
                        act.activation(t_z[:, cols], rz[c][:, CW:2 * CW], ACT.Tanh, scale=half_unscale[:],
                                       bias=b_half[:, 1:2]).then_inc(z_sb.sem, 1)

                begin(0)
                gates(0)
                if ahead:
                    copy_out(xT[:], slot["xT"][:], xT_ps, far, xT_sb)

                def first_part(i):
                    if ahead:
                        for x in stacked:
                            act.wait_ge(x.sem, x.after(nxt, heads))
                        copy_out(parts[i][:, 0], slot["qk", i][:], qk_ps[i], far, part1[i])

                begin(1)
                first_part(0)
                gates(1)
                first_part(1)
                begin(2)
                if tail:
                    copy_out(x2T[:], slot["x2T"][:], x2T_ps, last, x2T_sb)
                gates(2)
                begin(3)
                if ahead:
                    copy_out(parts[0][:, 3], rest[0][:], rest1[0], far, part2[0])
                gates(3)
                if ahead:
                    copy_out(parts[1][:, 1], rest[1][:], rest1[1], far, part2[1])
                    act.wait_ge(o_ps.sem, o_ps.after(t, G))
                    copy_out(v1[lane][:, :, :, 0:dh], slot["v"][:].rearrange("p (g h d) -> p g h d", g=G, d=dh),
                             v_ps, far, v_sb)
                begin(4)
                if head:
                    act.wait_ge(adj3_sb.sem, adj3_sb.after(last))
                    copy_out(adjT[other][:], slot["adjT"][:].rearrange("p (g n) -> p g n", g=G),
                             adjT_ps, nxt, adjT_sb)
                gates(4)
                exps([0])
                begin(5)
                exps([1, 2])
                gates(5)
                exps([3])
                begin(6)
                exps([4, 5])
                gates(6)
                exps([6])
                begin(7)
                if tail:
                    copy_out(hsT[:], slot["hs"][:], hs_ps, last, hs_sb)
                exps([7])
                gates(7)
                if tail:
                    copy_out(hid[:, 0], slot["hid", 0][:], hid_ps, last, hid_sb, 1, b31[:, 0:1], ACT.Relu)
                begin(8)
                if tail:
                    copy_out(hid[:, 1], slot["hid", 1][:], hid_ps, last, hid_sb, 2, b31[:, 1:2], ACT.Relu)
                if head:
                    copy_out(oT[:], slot["oT"][:], oT_ps, nxt, oT_sb)
                gates(8)
                begin(9)
                gates(9)
                if own:
                    candidate(9)
                if head:
                    act.wait_ge(hT_ps.sem, hT_ps.after(last))
                    copy_out(hT[other][:], slot["h0"][:], h0_ps, nxt, h0_sb)

            halves(act, half)

        @block.vector
        def _(dve):
            dve.wait_ge(s_const, 16 * len(loads))
            dve.tensor_scalar(wq[:], wq[:], float(dh) ** -0.5, None, ALU.mult).then_inc(s_dve0, 1)
            dve.tensor_tensor(b_half[:, 0:2], b_ih[:, 0:2], b_hh[:, 0:2], ALU.add).then_inc(s_dve0, 1)
            dve.tensor_scalar(b_half[:, 2:3], b_hh[:, 2:3], 0.5, None, ALU.mult).then_inc(s_dve0, 1)
            dve.tensor_scalar(eps3[:], eps3[:], 1.0, None, ALU.add).then_inc(s_dve0, 1)
            dve.wait_ge(s_dve0, 4)
            dve.tensor_scalar(b_half[:, 0:2], b_half[:, 0:2], 0.5, None, ALU.mult).then_inc(s_dve0, 1)
            dve.wait_ge(s_pool0, 9)
            dve.tensor_copy(ident16[:], ident[:]).then_inc(s_dve0, 1)
            dve.tensor_scalar(eps_ident[:], ident[:], eps3[:, 0:1], None, ALU.mult).then_inc(s_dve0, 1)
            for l in range(layers):
                dve.wait_ge(s_pe0, l + 1)
                dve.tensor_copy(w_in[:, l], bank[l % 2][:, 0:3 * P]).then_inc(s_dve0, 1)
            dve.wait_ge(s_dve0, 7 + layers)
            all_in = w_in[:].rearrange("p l n -> p (l n)")
            for i, w in enumerate((w_hh[:], all_in)):
                dve.tensor_reduce(extremes[:, i:i + 1], w, AX_X, ALU.max)
                ins = dve.tensor_reduce(extremes[:, 2 + i:3 + i], w, AX_X, ALU.min)
            chain = signal_chain(dve, ctx.enter_context(nc.semaphore("dve_weights")))
            chain(ins)
            chain(dve.tensor_scalar(extremes[:, 2:4], extremes[:, 2:4], -1.0, None, ALU.mult))
            dve.tensor_reduce(w_rec[:], extremes[:], AX_X, ALU.max).then_inc(s_dve0, 1)
            dve.wait_ge(s_pool0, 10)
            chain(dve.tensor_scalar(w_max[:], w_max[:], 1e-30, None, ALU.max))
            chain(dve.tensor_scalar(w_pow[:].bitcast(I32), w_max[:].bitcast(I32), 0x7F800000, None, ALU.bitwise_and))
            chain(dve.reciprocal(w_rec[:], w_pow[:]))
            dve.tensor_scalar(s_hh[:], w_rec[:], W_TOP, None, ALU.mult)
            dve.tensor_scalar(s_in[:], w_rec[:], W_TOP * H_SCALE / AGG_SCALE, None, ALU.mult)
            dve.tensor_scalar(unscale[:], w_pow[:], 1.0 / (W_TOP * H_SCALE), None, ALU.mult)
            chain(dve.tensor_scalar(half_unscale[:], w_pow[:], 0.5 / (W_TOP * H_SCALE), None, ALU.mult))
            high_in, low_in = (w_in16[:, c].rearrange("p l n -> p (l n)") for c in range(2))
            dve.tensor_scalar(w_hh16[:, 0], w_hh[:], s_hh[:], None, ALU.mult)
            chain(dve.tensor_scalar(high_in, all_in, s_in[:], None, ALU.mult))
            dve.scalar_tensor_tensor(w_hh16[:, 1], w_hh[:], s_hh[:], w_hh16[:, 0], ALU.mult, ALU.subtract)
            chain(dve.scalar_tensor_tensor(low_in, all_in, s_in[:], high_in, ALU.mult, ALU.subtract))
            dve.sem_inc(s_start, 1)

            def norm_stats(grp, n):
                i = min(n, 1)
                dve.wait_ge(t_sb[n].sem, t_sb[n].after(grp))
                for g in range(G):
                    ins = dve.bn_stats(stats[i][:, g], t_ln[i][:, g])
                ins.then_inc(stats_sb[n].sem, 1)
                dve.wait_ge(s_const, 16)
                dve.wait_ge(stats_sb[n].sem, stats_sb[n].after(grp))
                for g in range(G):
                    ins = dve.bn_aggr(mean_var[i][:, g], stats[i][:, g])
                ins.then_inc(var_sb[n].sem, 1)

            def norm_apply(grp, n, dst):
                i = min(n, 1)
                dve.wait_ge(rstd_sb[n].sem, rstd_sb[n].after(grp))
                for g in range(G):
                    ins = dve.tensor_scalar(dst[:, g], t_ln[i][:, g], mean_var[i][:, g, 0:1],
                                            rstd[i][:, g:g + 1], ALU.subtract, ALU.mult)
                ins.then_inc(ln_sb[n].sem, 1)

            def half(t, lane, ahead, head, own, tail):
                far, nxt, last, other = t.plus(2), t.plus(1), t.plus(-1), 1 - lane
                slot = banks_of()

                def split(s):
                    l, c, k, cols = step(s)
                    state = hT[lane][:, cols]
                    dve.tensor_scalar(h16[:, 0, cols], state, H_SCALE, None, ALU.mult).then_inc(hhi_sb.sem, 1)
                    dve.wait_ge(hhi_sb.sem, hhi_sb.after(t, k))
                    dve.scalar_tensor_tensor(h16[:, 1, cols], state, H_SCALE, h16[:, 0, cols], ALU.mult,
                                             ALU.subtract).then_inc(hlo_sb.sem, 1)

                def first_state():
                    for c in range(CHAINS):
                        gs = slice(c * CG, (c + 1) * CG)
                        dve.wait_ge(ln_sb[0].sem, ln_sb[0].after(t))
                        dve.wait_ge(agg_ps.sem, agg_ps.after(last, steps))
                        dve.tensor_scalar(hn16[:, 0, gs], x1[lane][:, gs], H_SCALE, None,
                                          ALU.mult).then_inc(nhi_sb.sem, 1)
                        dve.wait_ge(nhi_sb.sem, nhi_sb.after(t, c + 1))
                        dve.scalar_tensor_tensor(hn16[:, 1, gs], x1[lane][:, gs], H_SCALE, hn16[:, 0, gs], ALU.mult,
                                                 ALU.subtract).then_inc(nlo_sb.sem, 1)
                        dve.wait_ge(h0_sb.sem, h0_sb.after(t))
                        split(c)

                def low(s):
                    l, c, k, cols = step(s)
                    if own:
                        dve.wait_ge(agghi_sb.sem, agghi_sb.after(t, k))
                        dve.scalar_tensor_tensor(agg16[:, 1, cols], ps_t[:, 0:CW], AGG_SCALE / H_SCALE,
                                                 agg16[:, 0, cols], ALU.mult, ALU.subtract).then_inc(agglo_sb.sem, 1)

                def gate(s):
                    l, c, k, cols = step(s)
                    if own:
                        dve.wait_ge(half_sb.sem, half_sb.after(t, k))
                        dve.wait_ge(r_sb.sem, r_sb.after(t, k))
                        dve.scalar_tensor_tensor(h_half[:, cols], t_r[:, cols], 1.0, h_half[:, cols], ALU.add,
                                                 ALU.mult).then_inc(gated_sb.sem, 1)
                        dve.wait_ge(gated_sb.sem, gated_sb.after(t, k))
                        dve.wait_ge(i_ps.sem, i_ps.after(t, k))
                        dve.scalar_tensor_tensor(pre[:, cols], hi[c][:, CW:2 * CW], unscale[:], h_half[:, cols],
                                                 ALU.mult, ALU.add).then_inc(pre_sb.sem, 1)

                def new_state(s):
                    l, c, k, cols = step(s)
                    if own:
                        dve.wait_ge(cand_sb.sem, cand_sb.after(t, k))
                        dve.tensor_tensor(diff[:, cols], hT[lane][:, cols], cand[:, cols],
                                          ALU.subtract).then_inc(diff_sb.sem, 1)
                        dve.wait_ge(diff_sb.sem, diff_sb.after(t, k))
                        dve.wait_ge(z_sb.sem, z_sb.after(t, k))
                        dve.scalar_tensor_tensor(diff[:, cols], t_z[:, cols], 1.0, diff[:, cols], ALU.add,
                                                 ALU.mult).then_inc(zdiff_sb.sem, 1)
                        dve.wait_ge(zdiff_sb.sem, zdiff_sb.after(t, k))
                        dve.scalar_tensor_tensor(hT[lane][:, cols], diff[:, cols], 0.5, cand[:, cols], ALU.mult,
                                                 ALU.add).then_inc(h_sb.sem, 1)
                        if l + 1 < layers:
                            dve.wait_ge(h_sb.sem, h_sb.after(t, k))
                            split(s + CHAINS)

                def maxes(*ids):
                    for i in ids if head else ():
                        c, g = i // G, i % G
                        dve.wait_ge(s_ps.sem, s_ps.after(nxt, i + 1))
                        dve.tensor_reduce(maxima[:, c * hc:(c + 1) * hc, g],
                                          slot["s", i][:].rearrange("p (h n) -> p h n", h=hc), AX_X,
                                          ALU.max).then_inc(max_sb.sem, 1)

                def probs(*ids):
                    for i in ids if head else ():
                        c, g = i % 2, i // 2
                        dve.wait_ge(exp_sb.sem, exp_sb.after(nxt, i + 1))
                        ev = e[g % 2][:, c * hc:(c + 1) * hc]
                        dve.scalar_tensor_tensor(ev, adjT[other][:, g].unsqueeze(1).to_broadcast([P, hc, P]),
                                                 ADJ_EPS, ev, ALU.add, ALU.mult).then_inc(prob_sb.sem, 1)

                def normalise(g):
                    if head:
                        o = slot["o", g][:, 0:heads * vw].rearrange("p (h w) -> p h w", w=vw)
                        dve.wait_ge(o_ps.sem, o_ps.after(nxt, g + 1))
                        dve.reciprocal(r_sum[g % 2][:], o[:, :, dh]).then_inc(rsum_sb.sem, 1)
                        dve.wait_ge(rsum_sb.sem, rsum_sb.after(nxt, g + 1))
                        dve.tensor_tensor(o_n[:, g], o[:, :, 0:dh],
                                          r_sum[g % 2][:].unsqueeze(2).to_broadcast([P, heads, dh]),
                                          ALU.mult).then_inc(norm_sb.sem, 1)

                def second_rest(i):
                    if ahead:
                        dve.wait_ge(part1[i].sem, part1[i].after(far))
                        dve.tensor_tensor(rest[i][:], slot["qk", i][:], parts[i][:, 0],
                                          ALU.subtract).then_inc(rest1[i].sem, 1)

                if own:
                    first_state()
                if tail:
                    dve.wait_ge(ln_sb[3].sem, ln_sb[3].after(last.plus(-1)))
                    dve.wait_ge(hT_ps.sem, hT_ps.after(last))
                    for g in range(G):
                        b = last.times(G, g)
                        ins = dve.scalar_tensor_tensor(
                            t_ln[1][:, g], slot["hT"][:, g * P:(g + 1) * P], nodemask[:, bass.ds(b, 1)],
                            x1[other][:, g], ALU.mult, ALU.add)
                    ins.then_inc(t_sb[1].sem, 1)
                low(0)
                if tail:
                    norm_stats(last, 1)
                maxes(0)

                gate(0)
                maxes(1)
                new_state(0)
                low(1)
                if tail:
                    norm_apply(last, 1, x2)
                maxes(2)

                gate(1)
                second_rest(0)
                maxes(3)
                new_state(1)
                second_rest(1)
                low(2)
                maxes(4)

                gate(2)
                maxes(5)
                new_state(2)
                maxes(6)
                low(3)
                maxes(7)
                if tail:
                    dve.wait_ge(h2_ps.sem, h2_ps.after(last))
                    dve.tensor_tensor(h2[:], slot["h2"][:].rearrange("p (g n) -> p g n", g=G),
                                      b2g[:].unsqueeze(1).to_broadcast([P, G, P]), ALU.add).then_inc(h2_sb.sem, 1)

                gate(3)
                if head:
                    dve.wait_ge(m_ps.sem, m_ps.after(nxt))
                    dve.wait_ge(m_stacked.sem, m_stacked.after(t, 3))
                    mT = slot["m"][0:heads * G, 0:P]
                    dve.tensor_copy(m_parts[:, 0], mT).then_inc(m1_sb.sem, 1)
                    dve.wait_ge(m1_sb.sem, m1_sb.after(nxt))
                    dve.tensor_tensor(m_rest[:], mT, m_parts[:, 0], ALU.subtract).then_inc(mr_sb.sem, 1)
                    dve.wait_ge(mr_sb.sem, mr_sb.after(nxt))
                    dve.tensor_copy(m_parts[:, 1], m_rest[:]).then_inc(m2_sb.sem, 1)
                    dve.wait_ge(m2_sb.sem, m2_sb.after(nxt))
                    dve.tensor_tensor(m_parts[:, 2], m_rest[:], m_parts[:, 1], ALU.subtract).then_inc(m3_sb.sem, 1)
                new_state(3)
                low(4)
                if tail:
                    dve.wait_ge(d2_ps.sem, d2_ps.after(last))
                    for g in range(G):
                        ins = dve.scalar_tensor_tensor(t_ln[1][:, g], slot["d2"][:, g * P:(g + 1) * P],
                                                       dis[other][:, g:g + 1], x2[:, g], ALU.mult, ALU.add)
                    ins.then_inc(t_sb[2].sem, 1)
                    norm_stats(last, 2)
                if head:
                    dve.wait_ge(adj_loaded.sem, adj_loaded.after(nxt))
                    dve.wait_ge(agg_ps.sem, agg_ps.after(last, steps))
                    dve.tensor_scalar(adj_on[other][:], adj[:], 0.0, None, ALU.not_equal).then_inc(adj_on_sb.sem, 1)
                    dve.wait_ge(off_sb.sem, off_sb.after(nxt))
                    dve.wait_ge(dis_sb.sem, dis_sb.after(t))
                    dve.reduce_sum(deg[:], adj_off[:], AX_X).then_inc(deg_sb.sem, 1)

                gate(4)
                probs(0)
                new_state(4)
                low(5)
                if tail:
                    norm_apply(last, 2, x3)
                probs(1, 2)

                gate(5)
                normalise(0)
                probs(3)
                new_state(5)
                probs(4)
                low(6)
                probs(5)
                normalise(1)

                gate(6)
                if ahead:
                    dve.tensor_copy(parts[0][:, 1:3], parts[0][:, 0:1].to_broadcast([P, 2, W]))
                    dve.wait_ge(part2[0].sem, part2[0].after(far))
                    dve.tensor_copy(parts[0][:, 4], parts[0][:, 3]).then_inc(copies[0].sem, 1)
                    dve.tensor_copy(parts[1][:, 5], parts[1][:, 0])
                    dve.wait_ge(part2[1].sem, part2[1].after(far))
                    dve.tensor_copy(parts[1][:, 3:5], parts[1][:, 0:2]).then_inc(copies[1].sem, 1)
                new_state(6)
                probs(6)
                low(7)
                normalise(2)
                probs(7)

                gate(7)
                normalise(3)
                new_state(7)
                low(8)

                gate(8)
                if head:
                    dve.wait_ge(y_ps.sem, y_ps.after(nxt))
                    dve.wait_ge(res0_sb.sem, res0_sb.after(nxt))
                    dve.tensor_tensor(t_ln[0][:], slot["y"][:].rearrange("p (g n) -> p g n", g=G), res0[other][:],
                                      ALU.add).then_inc(t_sb[0].sem, 1)
                new_state(8)
                if head:
                    norm_stats(nxt, 0)
                low(9)
                if tail:
                    dve.wait_ge(y3_ps.sem, y3_ps.after(last))
                    dve.wait_ge(res3_sb.sem, res3_sb.after(last))
                    dve.tensor_tensor(t_ln[1][:], slot["y3"][:].rearrange("p (g n) -> p g n", g=G), res3[:],
                                      ALU.add).then_inc(t_sb[3].sem, 1)
                if head:
                    norm_apply(nxt, 0, x1[other])
                gate(9)
                if tail:
                    norm_stats(last, 3)
                new_state(9)
                if tail:
                    dve.wait_ge(stored.sem, stored.after(last.plus(-1)))
                    norm_apply(last, 3, x4)

            halves(dve, half)

        @block.tensor
        def _(pe):
            pe.wait_ge(s_const, 16 * len(loads))
            for l in range(layers):
                if l >= 2:
                    pe.wait_ge(s_dve0, 7 + l - 1)
                pe.matmul(bank[l % 2][:, 0:3 * P], w_l[:, l], w_ih[:], start=True, stop=True).then_inc(s_pe0, 1)
            pe.wait_ge(s_start, 1)

            def turn(dst, src, done, idn=ident):
                for g in range(G):
                    ins = pe.transpose(dst[:, g * P:(g + 1) * P], src[:, g * P:(g + 1) * P], idn[:])
                ins.then_inc(done.sem, 1)

            def flat(a):
                return a[:].rearrange("p g n -> p (g n)")

            def per_graph(dst, lhs, rhs, done):
                for g in range(G):
                    ins = pe.matmul(dst[:, g * P:(g + 1) * P], lhs(g), rhs(g), start=True, stop=True)
                ins.then_inc(done.sem, 1)

            def blk(a):
                return lambda g: a[:, g * P:(g + 1) * P]

            def row(a):
                return lambda g: a[:, g]

            def half(t, lane, ahead, head, own, tail):
                far, nxt, last, other = t.plus(2), t.plus(1), t.plus(-1), 1 - lane
                runs = {2: ahead, 1: head, 0: own, -1: tail}
                after_full_half = t.a or 1 < t.b <= groups - 2

                def take(name):
                    n = next(i for i, p in enumerate(pieces) if p[0] == name)
                    assert runs[pieces[n][1]]
                    m = n - len(ring)
                    while m >= 0 and not runs[pieces[m][1]]:
                        m -= len(ring)
                    if m >= 0:
                        _, off, read, k = pieces[m]
                        pe.wait_ge(read.sem, read.after(t.plus(off), k))
                    elif after_full_half:
                        m = max(i for i in range(len(pieces)) if i % len(ring) == n % len(ring))
                        _, off, read, k = pieces[m]
                        pe.wait_ge(read.sem, read.after(t.plus(off - 1), k))
                    return ring[n % len(ring)]

                def leave():
                    for b in range(len(ring)):
                        used = [p for i, p in enumerate(pieces) if i % len(ring) == b and runs[p[1]]]
                        if used:
                            _, off, read, k = used[-1]
                            pe.wait_ge(read.sem, read.after(t.plus(off), k))

                def scores(name, i, c, g, a, b, rows, done):
                    dst = take((name, i))
                    for j in range(hc):
                        ins = pe.matmul(dst[:, j * P:(j + 1) * P],
                                        stack[a][0:rows, other, c * hc + j, g * P:(g + 1) * P],
                                        stack[b][0:rows, other, c * hc + j, g * P:(g + 1) * P], start=True, stop=True)
                    ins.then_inc(done.sem, 1)

                def query_rows(*ids):
                    for i in ids if head else ():
                        c, g = i // G, i % G
                        if g == 0:
                            pe.wait_ge(stacked[c].sem, stacked[c].after(nxt, heads))
                        scores("s", i, c, g, 0, 1, KS, s_ps)

                def key_rows(*ids):
                    for i in ids if head else ():
                        if i == 0:
                            pe.wait_ge(m_stacked.sem, m_stacked.after(nxt, 3))
                        scores("st", i, i % 2, i // 2, 1, 0, KS + 3, st_ps)

                def attend(g):
                    if head:
                        dst = take(("o", g))
                        pe.wait_ge(prob_sb.sem, prob_sb.after(nxt, 2 * g + 2))
                        for h in range(heads):
                            ins = pe.matmul(dst[:, h * vw:(h + 1) * vw], e[g % 2][:, h], v1[other][:, g, h],
                                            start=True, stop=True)
                        ins.then_inc(o_ps.sem, 1)

                def gate_parts(dst, w, gate, x, start, stop):
                    cols = slice(gate * P, (gate + 1) * P)
                    for n, (a, b) in enumerate(((0, 0), (0, 1), (1, 0))):
                        ins = pe.matmul(dst, w(a)[:, cols], x(b), start=(start and n == 0), stop=(stop and n == 2))
                    return ins

                def hidden(s):
                    l, c, k, cols = step(s)
                    pe.wait_ge(hlo_sb.sem, hlo_sb.after(t, k))
                    pe.wait_ge(agglo_sb.sem, agglo_sb.after(t, k - 1))
                    if l:
                        for a in range(2):
                            for g in range(CG):
                                n = a * CG + g
                                ins = pe.transpose(ps_t16[:, n * P:(n + 1) * P],
                                                   h16[:, a, (c * CG + g) * P:(c * CG + g + 1) * P], ident16[:])
                        ins.then_inc(hn_ps.sem, 1)
                    pe.wait_ge(z_sb.sem, z_sb.after(t, k - CHAINS))
                    pe.wait_ge(pre_sb.sem, pre_sb.after(t, k - CHAINS))
                    w, x = (lambda a: w_hh16[:, a]), (lambda b: h16[:, b, cols])
                    gate_parts(rz[c][:, 0:CW], w, 0, x, True, False)
                    gate_parts(rz[c][:, CW:2 * CW], w, 1, x, False, False)
                    gate_parts(hi[c][:, 0:CW], w, 2, x, True, True).then_inc(hh_ps.sem, 1)

                def neighbours(s):
                    l, c, k, cols = step(s)
                    if l:
                        pe.wait_ge(hn_sb.sem, hn_sb.after(t, k - CHAINS))
                    else:
                        pe.wait_ge(nlo_sb.sem, nlo_sb.after(t, k))
                    for g in range(CG):
                        for a in range(2):
                            ins = pe.matmul(ps_t[:, g * P:(g + 1) * P], hn16[:, a, c * CG + g],
                                            adj_on[lane][:, c * CG + g], start=(a == 0), stop=(a == 1))
                    ins.then_inc(agg_ps.sem, 1)

                def begin(s):
                    if own:
                        hidden(s)
                        neighbours(s)

                def inputs_in(s):
                    l, c, k, cols = step(s)
                    if own:
                        pe.wait_ge(agglo_sb.sem, agglo_sb.after(t, k))
                        w, x = (lambda a: w_in16[:, a, l]), (lambda b: agg16[:, b, cols])
                        gate_parts(rz[c][:, 0:CW], w, 0, x, False, False)
                        gate_parts(rz[c][:, CW:2 * CW], w, 1, x, False, True).then_inc(rz_ps.sem, 1)
                        pe.wait_ge(half_sb.sem, half_sb.after(t, k))
                        gate_parts(hi[c][:, CW:2 * CW], w, 2, x, True, True).then_inc(i_ps.sem, 1)

                def project(i):
                    if ahead:
                        dst = take(("qk", i))
                        pe.wait_ge(xT_sb.sem, xT_sb.after(far))
                        pe.matmul(dst[:], (wq, wk)[i][:], xT[:], start=True, stop=True).then_inc(qk_ps[i].sem, 1)

                def first_dense(h):
                    if tail:
                        b = take(("hid", h))
                        pe.wait_ge(hs_sb.sem, hs_sb.after(last))
                        pe.matmul(b[:], w31[:, h * P:(h + 1) * P], hsT[:], start=True, stop=True).then_inc(hid_ps.sem, 1)

                begin(0)
                if tail:
                    b = take("hT")
                    pe.wait_ge(h_sb.sem, h_sb.after(last, steps))
                    turn(b, hT[other], hT_ps)
                query_rows(0)
                inputs_in(0)
                if ahead:
                    b = take("xT")
                    pe.wait_ge(x_loaded.sem, x_loaded.after(far))
                    turn(b, flat(x_in), xT_ps)
                query_rows(1)

                begin(1)
                query_rows(2)
                project(0)
                inputs_in(1)
                project(1)
                query_rows(3)

                begin(2)
                if tail:
                    b = take("x2T")
                    pe.wait_ge(ln_sb[1].sem, ln_sb[1].after(last))
                    turn(b, flat(x2), x2T_ps)
                query_rows(4)
                inputs_in(2)
                query_rows(5, 6)

                begin(3)
                query_rows(7)
                if tail:
                    b = take("h2")
                    pe.wait_ge(x2T_sb.sem, x2T_sb.after(last))
                    per_graph(b, blk(x2T), lambda g: w2g[:], h2_ps)
                inputs_in(3)
                if ahead:
                    per_graph(take("v"), blk(xT), lambda g: wv[:], v_ps)
                if head:
                    b = take("m")
                    pe.wait_ge(max_sb.sem, max_sb.after(nxt, 2 * G))
                    pe.transpose(b[0:heads * G, 0:P], maxima[:].rearrange("p h g -> p (h g)"),
                                 ident[:]).then_inc(m_ps.sem, 1)

                begin(4)
                if head:
                    b = take("adjT")
                    pe.wait_ge(adj_loaded.sem, adj_loaded.after(nxt))
                    turn(b, flat(adj), adjT_ps)
                if tail:
                    b = take("d2")
                    pe.wait_ge(h2_sb.sem, h2_sb.after(last))
                    pe.wait_ge(adj2_sb.sem, adj2_sb.after(last))
                    per_graph(b, row(adj2[other]), row(h2), d2_ps)
                inputs_in(4)
                key_rows(0, 1)

                begin(5)
                key_rows(2)
                attend(0)
                inputs_in(5)
                key_rows(3, 4)

                begin(6)
                attend(1)
                key_rows(5)
                inputs_in(6)
                key_rows(6)
                if tail:
                    b = take("hs")
                    pe.wait_ge(ln_sb[2].sem, ln_sb[2].after(last))
                    pe.wait_ge(adj3_sb.sem, adj3_sb.after(last))
                    per_graph(b, row(x3), row(adj3[other]), hs_ps)

                begin(7)
                attend(2)
                key_rows(7)
                inputs_in(7)
                first_dense(0)
                attend(3)

                begin(8)
                first_dense(1)
                if head:
                    b = take("oT")
                    pe.wait_ge(norm_sb.sem, norm_sb.after(nxt, G))
                    turn(b, o_n[:].rearrange("p g h d -> p (g h d)"), oT_ps)
                inputs_in(8)
                if head:
                    b = take("y")
                    pe.wait_ge(oT_sb.sem, oT_sb.after(nxt))
                    per_graph(b, blk(oT), lambda g: wo[:], y_ps)

                begin(9)
                if tail:
                    b = take("y3")
                    pe.wait_ge(hid_sb.sem, hid_sb.after(last, 2))
                    for g in range(G):
                        for h in range(2):
                            ins = pe.matmul(b[:, g * P:(g + 1) * P], hid[:, h, g * P:(g + 1) * P], w32[:, h],
                                            start=(h == 0), stop=(h == 1))
                    ins.then_inc(y3_ps.sem, 1)
                inputs_in(9)
                if head:
                    b = take("h0")
                    pe.wait_ge(ln_sb[0].sem, ln_sb[0].after(nxt))
                    turn(b, flat(x1[other]), h0_ps)
                if not (ahead and head and own and tail):
                    leave()

            halves(pe, half)


def signal_chain(engine, sem):
    done = [0]

    def link(ins):
        done[0] += 1
        ins.then_inc(sem, 1)
        engine.wait_ge(sem, done[0])

    return link


def kernel(**inputs):
    import numpy as np
    import concourse.bacc as bacc
    from concourse.bass_utils import run_bass_kernel_spmd

    a = {n: np.asarray(v) for n, v in inputs.items()}
    lay = {
        "x": a["x"], "adj": a["adj"], "nodemask_T": a["nodemask"].T,
        "L0_Wq_T": a["L0_gnn_Wq"].T, "L0_Wk_T": a["L0_gnn_Wk"].T, "L0_Wv_T": a["L0_gnn_Wv"].T,
        "L0_Wo_T": a["L0_gnn_Wo"].T, "L0_bo": a["L0_gnn_bo"].reshape(1, -1),
        "L1_weight_T": a["L1_gnn_weight"].transpose(0, 2, 1),
        "L1_w_ih_T": a["L1_gnn_w_ih"].T, "L1_w_hh_T": a["L1_gnn_w_hh"].T,
        "L1_b_ih": a["L1_gnn_b_ih"].reshape(3, -1).T, "L1_b_hh": a["L1_gnn_b_hh"].reshape(3, -1).T,
        "L2_W_T": a["L2_gnn_W"].T, "L2_b": a["L2_gnn_b"].reshape(1, -1),
        "L3_eps": a["L3_gnn_eps"].reshape(1, 1), "L3_W1": a["L3_gnn_W1"],
        "L3_b1": a["L3_gnn_b1"].reshape(2, -1).T, "L3_W2": a["L3_gnn_W2"],
        "L3_b2": a["L3_gnn_b2"].reshape(1, -1),
    }
    nc = bacc.Bacc("TRN2", target_bir_lowering=False, num_devices=1)
    arrays, aps = {}, {}
    for name, v in lay.items():
        v = np.ascontiguousarray(v)
        arrays[f"in_{name}"] = v
        aps[name] = nc.dram_tensor(f"in_{name}", v.shape, mybir.dt.from_np(v.dtype), kind="ExternalInput").ap()
    out = nc.dram_tensor("out", a["x"].shape, F32, kind="ExternalOutput").ap()
    gnn_stack(nc, aps, out)
    r = run_bass_kernel_spmd(nc, [arrays], core_ids=[0])
    return r.results[0]["out"]
```

```python
from contextlib import ExitStack

import concourse.bass as bass
from concourse import mybir

F32 = mybir.dt.float32
BF16 = mybir.dt.bfloat16
F16 = mybir.dt.float16
I32 = mybir.dt.int32
ALU = mybir.AluOpType
ACT = mybir.ActivationFunctionType
AX_X = mybir.AxisListType.X
RMAX = bass.bass_isa.ReduceOp.max

P = 128
G = 4
W = G * P
CHAINS = 2
CG = G // CHAINS
CW = CG * P
LANES = 2
LN_EPS = 1e-5
ADJ_EPS = 1e-6

H_SCALE = 2.0 ** 11
AGG_SCALE = 2.0 ** 5
W_TOP = 2.0 ** 8

TERMS = [(0, 0), (0, 1), (0, 2), (1, 0), (1, 1), (2, 0)]
NT = len(TERMS)


class Group:

    def __init__(self, rnd, a, b):
        self.rnd, self.a, self.b = rnd, a, b

    def plus(self, n):
        return Group(self.rnd, self.a, self.b + n)

    def times(self, m, plus):
        c = self.b * m + plus
        return self.rnd * (self.a * m) + c if self.a else c


class Signal:

    AHEAD = 2

    def __init__(self, sem, per_group=1, unit=1):
        self.sem, self.per_group, self.unit = sem, per_group, unit

    def after(self, group, k=1):
        step = self.per_group * self.unit
        return group.times(step, self.AHEAD * step + k * self.unit)


def gnn_stack(nc, t, out):
    B, N, D = t["x"].shape
    assert N == P and D == P
    heads = 8
    dh = D // heads
    hc = heads // 2
    layers = t["L1_weight_T"].shape[0]
    groups = B // G
    vw = dh + 1
    KS = NT * dh
    assert groups % 2 == 0 and CHAINS * layers == 10

    with ExitStack() as ctx:
        def sb(name, shape, dt=F32):
            return ctx.enter_context(nc.sbuf_tensor(name, shape, dt))

        def signal(name, per_group=1, unit=1):
            s = Signal(ctx.enter_context(nc.semaphore(name)), per_group, unit)
            signals.append(s)
            return s

        signals = []
        bank = [ctx.enter_context(nc.psum_tensor(f"bank{i}", [P, W], F32)) for i in range(8)]
        rz, hi, ps_t = bank[0:2], bank[2:4], bank[4]
        ring = bank[5:]
        ps_t16 = ps_t[:].bitcast(F16)

        ident = sb("ident", [P, P])
        ident16 = sb("ident16", [P, P], F16)
        off_diag = sb("off_diag", [P, P])
        eps_ident = sb("eps_ident", [P, P])
        wq = sb("wq", [P, P])
        wk = sb("wk", [P, P])
        wv = sb("wv", [P, P])
        wo = sb("wo", [P, P])
        bo = sb("bo", [P, P])
        w_l = sb("w_l", [P, layers, P])
        w_ih = sb("w_ih", [P, 3 * P])
        w_hh = sb("w_hh", [P, 3 * P])
        w_in = sb("w_in", [P, layers, 3 * P])
        w_hh16 = sb("w_hh16", [P, 2, 3 * P], F16)
        w_in16 = sb("w_in16", [P, 2, layers, 3 * P], F16)
        extremes = sb("extremes", [P, 4])
        w_max = sb("w_max", [P, 1])
        w_pow = sb("w_pow", [P, 1])
        w_rec = sb("w_rec", [P, 1])
        s_hh = sb("s_hh", [P, 1])
        s_in = sb("s_in", [P, 1])
        unscale = sb("unscale", [P, 1])
        half_unscale = sb("half_unscale", [P, 1])
        b_ih = sb("b_ih", [P, 3])
        b_hh = sb("b_hh", [P, 3])
        b_half = sb("b_half", [P, 3])
        w2g = sb("w2g", [P, P])
        b2g = sb("b2g", [P, P])
        w31 = sb("w31", [P, 2 * P])
        b31 = sb("b31", [P, 2])
        w32 = sb("w32", [P, 2, P])
        b32 = sb("b32", [P, P])
        eps3 = sb("eps3", [P, 1])
        nodemask = sb("nodemask", [P, B])
        power = sb("power", [P, G])
        ln_eps = sb("ln_eps", [P, G])
        minus = sb("minus", [P, G])
        ones = sb("ones", [1, P])

        def lanes(name, shape, dt=F32):
            return [sb(f"{name}{i}", shape, dt) for i in range(LANES)]

        x_in = sb("x_in", [P, G, P])
        adj = sb("adj", [P, G, P])
        adj_off = sb("adj_off", [P, G, P])
        adjT = lanes("adjT", [P, G, P])
        adj_on = lanes("adj_on", [P, G, P], F16)
        deg = sb("deg", [P, G])
        dis = lanes("dis", [P, G])
        xT = sb("xT", [P, W])
        parts = [sb(f"{n}_parts", [P, NT, W], BF16) for n in "qk"]
        rest = [sb(f"{n}_rest", [P, W]) for n in "qk"]
        stack = [sb(f"{n}_stack", [P, LANES, heads, W], BF16) for n in "qk"]
        v1 = lanes("v1", [P, G, heads, vw])
        maxima = sb("maxima", [P, heads, G])
        m_parts = sb("m_parts", [heads * G, 3, P], BF16)
        m_rest = sb("m_rest", [heads * G, P])
        e = [sb(f"e{i}", [P, heads, P]) for i in range(2)]
        r_sum = [sb(f"r_sum{i}", [P, heads]) for i in range(2)]
        o_n = sb("o_n", [P, G, heads, dh])
        oT = sb("oT", [P, W])
        res0 = lanes("res0", [P, G, P])
        t_ln = [sb(f"t_ln{i}", [P, G, P]) for i in range(2)]
        stats = [sb(f"stats{i}", [P, G, 6]) for i in range(2)]
        mean_var = [sb(f"mean_var{i}", [P, G, 2]) for i in range(2)]
        var_eps = [sb(f"var_eps{i}", [P, G]) for i in range(2)]
        rstd = [sb(f"rstd{i}", [P, G]) for i in range(2)]
        minus_mean = [sb(f"minus_mean{i}", [P, G]) for i in range(2)]
        shift = [sb(f"shift{i}", [P, G]) for i in range(2)]
        x1 = lanes("x1", [P, G, P])
        hT = lanes("hT", [P, W])
        h16 = sb("h16", [P, 2, W], F16)
        hn16 = sb("hn16", [P, 2, G, P], F16)
        agg16 = sb("agg16", [P, 2, W], F16)
        t_r = sb("t_r", [P, W])
        t_z = sb("t_z", [P, W])
        h_half = sb("h_half", [P, W])
        pre = sb("pre", [P, W])
        cand = sb("cand", [P, W])
        kept = sb("kept", [P, W])
        renewed = sb("renewed", [P, W])
        adj2 = lanes("adj2", [P, G, P])
        adj3 = lanes("adj3", [P, G, P])
        x2 = sb("x2", [P, G, P])
        x2T = sb("x2T", [P, W])
        h2 = sb("h2", [P, G, P])
        x3 = sb("x3", [P, G, P])
        hsT = sb("hsT", [P, W])
        hid = sb("hid", [P, 2, W])
        res3 = sb("res3", [P, G, P])
        x4 = sb("x4", [P, G, P])

        s_const = ctx.enter_context(nc.semaphore("const_loaded"))
        s_pool0 = ctx.enter_context(nc.semaphore("pool_setup"))
        s_dve0 = ctx.enter_context(nc.semaphore("dve_setup"))
        s_pe0 = ctx.enter_context(nc.semaphore("pe_setup"))
        s_start = ctx.enter_context(nc.semaphore("setup_done"))
        x_loaded = signal("x_loaded", 1, 16)
        adj_loaded = signal("adj_loaded", 1, 16)
        stacked = [signal(f"stacked{c}", heads, 16) for c in range(2)]
        m_stacked = signal("m_stacked", 3, 16)
        stored = signal("stored", 1, 16)
        adjT_ps, adjT_sb = signal("adjT_ps"), signal("adjT_sb")
        xT_ps, xT_sb = signal("xT_ps"), signal("xT_sb")
        qk_ps = [signal("q_ps"), signal("k_ps")]
        part1 = [signal("q_part1"), signal("k_part1")]
        rest1 = [signal("q_rest1"), signal("k_rest1")]
        part2 = [signal("q_part2"), signal("k_part2")]
        part3 = [signal("q_part3"), signal("k_part3")]
        copies = [signal("q_copies"), signal("k_copies")]
        v_ps, v_sb = signal("v_ps"), signal("v_sb")
        adj_on_sb = signal("adj_on_sb")
        off_sb, deg_sb, dis_sb = signal("off_sb"), signal("deg_sb"), signal("dis_sb")
        res0_sb, res3_sb = signal("res0_sb"), signal("res3_sb")
        adj2_sb, adj3_sb = signal("adj2_sb"), signal("adj3_sb")
        s_ps, max_sb = signal("s_ps", 2 * G), signal("max_sb", 2 * G)
        m_ps, m1_sb, mr_sb, m2_sb, m3_sb = (signal(n) for n in ("m_ps", "m1_sb", "mr_sb", "m2_sb", "m3_sb"))
        st_ps, exp_sb, prob_sb = signal("st_ps", 2 * G), signal("exp_sb", 2 * G), signal("prob_sb", 2 * G)
        o_ps, rsum_sb, norm_sb = signal("o_ps", G), signal("rsum_sb", G), signal("norm_sb", G)
        oT_ps, oT_sb, y_ps = signal("oT_ps"), signal("oT_sb"), signal("y_ps")
        t_sb = [signal(f"t_sb{n}") for n in range(4)]
        stats_sb = [signal(f"stats_sb{n}") for n in range(4)]
        var_sb = [signal(f"var_sb{n}") for n in range(4)]
        vareps_sb = [signal(f"vareps_sb{n}") for n in range(4)]
        rstd_sb = [signal(f"rstd_sb{n}") for n in range(4)]
        mmean_sb, shift_sb = ([signal(f"{a}{n}") for n in range(3)] for a in ("mmean_sb", "shift_sb"))
        centred_sb = signal("centred_sb")
        ln_sb = [signal(f"ln_sb{n}", G) for n in range(4)]
        h0_ps, h0_sb = signal("h0_ps"), signal("h0_sb")
        steps = CHAINS * layers
        h_sb = signal("h_sb", steps)
        hhi_sb, hlo_sb = signal("hhi_sb", steps), signal("hlo_sb", steps)
        nhi_sb, nlo_sb = signal("nhi_sb", CHAINS), signal("nlo_sb", CHAINS)
        hn_ps, hn_sb = signal("hn_ps", steps - CHAINS), signal("hn_sb", steps - CHAINS)
        agg_ps, agghi_sb, agglo_sb = (signal(n, steps) for n in ("agg_ps", "agghi_sb", "agglo_sb"))
        hh_ps, rz_ps, i_ps = (signal(n, steps) for n in ("hh_ps", "rz_ps", "i_ps"))
        half_sb, r_sb, z_sb = (signal(n, steps) for n in ("half_sb", "r_sb", "z_sb"))
        gated_sb, pre_sb, cand_sb = (signal(n, steps) for n in ("gated_sb", "pre_sb", "cand_sb"))
        kept_sb, new_sb = (signal(n, steps) for n in ("kept_sb", "new_sb"))
        hT_ps = signal("hT_ps")
        x2T_ps, x2T_sb = signal("x2T_ps"), signal("x2T_sb")
        h2_ps, h2_sb, d2_ps = signal("h2_ps"), signal("h2_sb"), signal("d2_ps")
        hs_ps, hs_sb = signal("hs_ps"), signal("hs_sb")
        hid_ps, hid_sb, y3_ps = signal("hid_ps", 2), signal("hid_sb", 2), signal("y3_ps")

        x_dram = t["x"].rearrange("b n d -> n b d")
        adj_dram = t["adj"].rearrange("b n m -> n b m")
        out_dram = out.rearrange("b n d -> n b d")

        loads = [
            (wq[:], t["L0_Wq_T"]), (wk[:], t["L0_Wk_T"]),
            (wv[:], t["L0_Wv_T"]), (wo[:], t["L0_Wo_T"]),
            (w_l[:], t["L1_weight_T"].rearrange("l e d -> e l d")),
            (w_ih[:], t["L1_w_ih_T"]), (w_hh[:], t["L1_w_hh_T"]),
            (b_ih[:], t["L1_b_ih"]), (b_hh[:], t["L1_b_hh"]),
            (w2g[:], t["L2_W_T"]), (w31[:], t["L3_W1"]), (b31[:], t["L3_b1"]),
            (w32[:], t["L3_W2"].rearrange("(c p) o -> p c o", p=P)),
            (nodemask[:], t["nodemask_T"]),
            (bo[:], t["L0_bo"].to_broadcast([P, P])), (b2g[:], t["L2_b"].to_broadcast([P, P])),
            (b32[:], t["L3_b2"].to_broadcast([P, P])), (eps3[:], t["L3_eps"].to_broadcast([P, 1])),
        ]

        released = {"hT": (-1, t_sb[1], 1), "xT": (2, xT_sb, 1), "x2T": (-1, x2T_sb, 1), "h2": (-1, h2_sb, 1),
                    "v": (2, v_sb, 1), "m": (1, mr_sb, 1), "adjT": (1, adjT_sb, 1), "d2": (-1, t_sb[2], 1),
                    "hs": (-1, hs_sb, 1), "oT": (1, oT_sb, 1), "y": (1, t_sb[0], 1), "y3": (-1, t_sb[3], 1),
                    "h0": (1, h0_sb, 1)}
        for i in range(2 * G):
            released["s", i] = (2 if i < 5 else 1, max_sb, i + 1)
            released["st", i] = (1, exp_sb, i + 1)
        for i in range(G):
            released["o", i] = (1, norm_sb, i + 1)
        for i in range(2):
            released["qk", i] = (2, rest1[i], 1)
            released["hid", i] = (-1, hid_sb, i + 1)
        order = [
            "xT", "adjT", ("s", 5), "hT", ("s", 6), ("s", 7), "m", ("qk", 0), ("qk", 1), ("st", 0),
            ("st", 1), "x2T", ("st", 2), "h2", ("st", 3), "d2", ("o", 0), ("st", 4), ("st", 5),
            ("st", 6), ("o", 1), ("st", 7), "hs", ("o", 2), ("hid", 0), ("o", 3), "oT", "v", "y",
            ("hid", 1), ("s", 0), ("s", 1), "y3", ("s", 2), ("s", 3), ("s", 4), "h0"]
        pieces = [(name, *released[name]) for name in order]

        def step(s):
            l, c = divmod(s, CHAINS)
            return l, c, s + 1, slice(c * CW, (c + 1) * CW)

        def banks_of():
            return {name: ring[n % len(ring)] for n, (name, *_) in enumerate(pieces)}

        def halves(engine, half):
            def fixed(n):
                runs = [0 <= n + off < groups for off in (2, 1, 0, -1)]
                half(Group(None, 0, n), n % LANES, *runs)

            for n in (-2, -1, 0):
                fixed(n)
            with engine.Fori(0, (groups - 4) // 2) as rnd:
                for n in (1, 2):
                    half(Group(rnd, 2, n), n % LANES, True, True, True, True)
            for n in range(groups - 3, groups + 1):
                fixed(n)

        block = ctx.enter_context(nc.Block())

        @block.sync
        def _(sp):
            for s in signals:
                sp.sem_inc(s.sem, s.AHEAD * s.per_group * s.unit)
            for dst, src in loads:
                sp.dma_start(dst, src).then_inc(s_const, 16)

            def load(dst, src, group, done):
                first = sp.snap(group.times(G, 0)) if group.a else group.times(G, 0)
                sp.dma_start(dst[:], src[:, bass.ds(first, G), :]).then_inc(done.sem, 16)

            load(x_in, x_dram, Group(None, 0, 0), x_loaded)

            def half(t, lane, ahead, head, own, tail):
                far, nxt, last, other = t.plus(2), t.plus(1), t.plus(-1), 1 - lane
                if head:
                    sp.wait_ge(s_pool0, 1)
                    sp.wait_ge(m3_sb.sem, m3_sb.after(nxt))
                    for i in range(3):
                        sp.dma_start(stack[0][KS + i:KS + i + 1, other].rearrange("p h (g n) -> p (h g) n", g=G),
                                     m_parts[:, i, :]).then_inc(m_stacked.sem, 16)
                if t.a or 0 <= t.b + 3 < groups:
                    sp.wait_ge(s_pool0, 1)
                    sp.wait_ge(xT_ps.sem, xT_ps.after(far))
                    sp.wait_ge(res0_sb.sem, res0_sb.after(far))
                    load(x_in, x_dram, t.plus(3), x_loaded)
                if ahead:
                    sp.wait_ge(s_pool0, 1)
                    sp.wait_ge(adjT_ps.sem, adjT_ps.after(nxt))
                    sp.wait_ge(adj_on_sb.sem, adj_on_sb.after(nxt))
                    sp.wait_ge(off_sb.sem, off_sb.after(nxt))
                    load(adj, adj_dram, far, adj_loaded)
                    sp.wait_ge(s_pool0, 1)
                    for i in range(2):
                        sp.wait_ge(part3[i].sem, part3[i].after(far))
                        sp.wait_ge(copies[i].sem, copies[i].after(far))
                    sp.wait_ge(s_pool0, 1)
                    sp.wait_ge(oT_ps.sem, oT_ps.after(t))
                    for h in range(heads):
                        for i in range(2):
                            sp.dma_start(stack[i][0:KS, lane, h, :],
                                         parts[i][h * dh:(h + 1) * dh]).then_inc(stacked[h // hc].sem, 16)
                if tail:
                    sp.wait_ge(s_pool0, 1)
                    sp.wait_ge(ln_sb[3].sem, ln_sb[3].after(last, G))
                    out_at = sp.snap(last.times(G, 0)) if t.a else last.times(G, 0)
                    sp.dma_start(out_dram[:, bass.ds(out_at, G), :], x4[:]).then_inc(stored.sem, 16)

            halves(sp, half)
            sp.wait_ge(stored.sem, 16 * (groups + Signal.AHEAD))

        @block.gpsimd
        def _(pool):
            pool.memset(ident[:], 0.0).then_inc(s_pool0, 1)
            pool.memset(off_diag[:], 1.0).then_inc(s_pool0, 1)
            pool.memset(power[:], -0.5).then_inc(s_pool0, 1)
            pool.memset(ln_eps[:], LN_EPS).then_inc(s_pool0, 1)
            pool.memset(minus[:], -1.0).then_inc(s_pool0, 1)
            pool.memset(ones[:], 1.0).then_inc(s_pool0, 1)
            for i in range(LANES):
                pool.memset(v1[i][:], 1.0).then_inc(s_pool0, 1)
            pool.wait_ge(s_pool0, 8)
            pool.memset(stack[1][KS:KS + 3], -1.0).then_inc(s_pool0, 1)
            pool.wait_ge(s_pool0, 9)
            pool.affine_select(out=ident[:], in_=ident[:], compare_op=ALU.not_equal, fill=1.0, base=0,
                               pattern=[[-1, P]], channel_multiplier=1).then_inc(s_pool0, 1)
            pool.affine_select(out=off_diag[:], in_=off_diag[:], compare_op=ALU.not_equal, fill=0.0, base=0,
                               pattern=[[-1, P]], channel_multiplier=1).then_inc(s_pool0, 1)
            pool.wait_ge(s_dve0, 8 + layers)
            pool.partition_all_reduce(w_max[:], w_rec[:], P, RMAX).then_inc(s_pool0, 1)
            pool.wait_ge(s_start, 1)

            def rsqrt(grp, n):
                i = min(n, 1)
                pool.wait_ge(var_sb[n].sem, var_sb[n].after(grp))
                pool.tensor_tensor(var_eps[i][:], mean_var[i][:, :, 1], ln_eps[:], ALU.add).then_inc(vareps_sb[n].sem, 1)
                if n < 3:
                    pool.tensor_tensor(minus_mean[i][:], mean_var[i][:, :, 0], minus[:],
                                       ALU.mult).then_inc(mmean_sb[n].sem, 1)
                pool.wait_ge(vareps_sb[n].sem, vareps_sb[n].after(grp))
                pool.tensor_tensor(rstd[i][:], var_eps[i][:], power[:], ALU.pow).then_inc(rstd_sb[n].sem, 1)
                if n < 3:
                    pool.wait_ge(mmean_sb[n].sem, mmean_sb[n].after(grp))
                    pool.wait_ge(rstd_sb[n].sem, rstd_sb[n].after(grp))
                    pool.tensor_tensor(shift[i][:], minus_mean[i][:], rstd[i][:], ALU.mult).then_inc(shift_sb[n].sem, 1)

            def half(t, lane, ahead, head, own, tail):
                far, nxt, last, other = t.plus(2), t.plus(1), t.plus(-1), 1 - lane

                def third_part(i):
                    if ahead:
                        pool.wait_ge(part2[i].sem, part2[i].after(far))
                        pool.tensor_tensor(parts[i][:, (5, 2)[i]], rest[i][:], parts[i][:, (3, 1)[i]],
                                           ALU.subtract).then_inc(part3[i].sem, 1)

                if head:
                    pool.wait_ge(adj_loaded.sem, adj_loaded.after(nxt))
                    pool.wait_ge(deg_sb.sem, deg_sb.after(t))
                    pool.tensor_tensor(adj_off[:], adj[:], off_diag[:].unsqueeze(1).to_broadcast([P, G, P]),
                                       ALU.mult).then_inc(off_sb.sem, 1)
                if own:
                    pool.wait_ge(adjT_sb.sem, adjT_sb.after(t))
                    pool.wait_ge(hs_ps.sem, hs_ps.after(t.plus(-2)))
                    pool.tensor_tensor(adj3[lane][:], adjT[lane][:],
                                       eps_ident[:].unsqueeze(1).to_broadcast([P, G, P]),
                                       ALU.add).then_inc(adj3_sb.sem, 1)
                if tail:
                    rsqrt(last, 1)
                if ahead:
                    pool.wait_ge(x_loaded.sem, x_loaded.after(far))
                    pool.wait_ge(t_sb[0].sem, t_sb[0].after(t))
                    pool.tensor_tensor(res0[lane][:], x_in[:], bo[:].unsqueeze(1).to_broadcast([P, G, P]),
                                       ALU.add).then_inc(res0_sb.sem, 1)
                third_part(0)
                if tail:
                    rsqrt(last, 2)
                third_part(1)
                if tail:
                    pool.wait_ge(ln_sb[2].sem, ln_sb[2].after(last, G))
                    pool.wait_ge(t_sb[3].sem, t_sb[3].after(last.plus(-1)))
                    pool.tensor_tensor(res3[:], x3[:], b32[:].unsqueeze(1).to_broadcast([P, G, P]),
                                       ALU.add).then_inc(res3_sb.sem, 1)
                if head:
                    rsqrt(nxt, 0)
                if head:
                    pool.wait_ge(deg_sb.sem, deg_sb.after(nxt))
                    pool.wait_ge(t_sb[2].sem, t_sb[2].after(last))
                    pool.tensor_tensor(dis[other][:], deg[:], power[:], ALU.pow).then_inc(dis_sb.sem, 1)
                if tail:
                    rsqrt(last, 3)
                if own:
                    pool.wait_ge(dis_sb.sem, dis_sb.after(t))
                    pool.wait_ge(adjT_sb.sem, adjT_sb.after(t))
                    pool.wait_ge(d2_ps.sem, d2_ps.after(t.plus(-2)))
                    pool.tensor_tensor(adj2[lane][:], adjT[lane][:],
                                       dis[lane][:].unsqueeze(2).to_broadcast([P, G, P]),
                                       ALU.mult).then_inc(adj2_sb.sem, 1)
                if tail:
                    pool.wait_ge(stored.sem, stored.after(last.plus(-1)))
                    pool.wait_ge(var_sb[3].sem, var_sb[3].after(last))
                    pool.tensor_tensor(x4[:], t_ln[1][:], mean_var[1][:, :, 0:1].to_broadcast([P, G, P]),
                                       ALU.subtract).then_inc(centred_sb.sem, 1)
                if tail:
                    pool.wait_ge(centred_sb.sem, centred_sb.after(last))
                    pool.wait_ge(rstd_sb[3].sem, rstd_sb[3].after(last))
                    pool.tensor_tensor(x4[:], x4[:], rstd[1][:].unsqueeze(2).to_broadcast([P, G, P]),
                                       ALU.mult).then_inc(ln_sb[3].sem, G)

            halves(pool, half)

        @block.scalar
        def _(act):
            act.wait_ge(s_start, 1)

            def copy_out(dst, src, ready, grp, done, k=1, bias=0.0, func=ACT.Identity):
                act.wait_ge(ready.sem, ready.after(grp, k))
                act.activation(dst, src, func, bias=bias).then_inc(done.sem, 1)

            def half(t, lane, ahead, head, own, tail):
                far, nxt, last, other = t.plus(2), t.plus(1), t.plus(-1), 1 - lane
                slot = banks_of()

                def exps(i):
                    if head:
                        c, g = i % 2, i // 2
                        if c == 0:
                            act.wait_ge(o_ps.sem, o_ps.after(nxt, g - 1))
                        act.wait_ge(st_ps.sem, st_ps.after(nxt, i + 1))
                        act.activation(e[g % 2][:, c * hc:(c + 1) * hc],
                                       slot["st", i][:].rearrange("p (h n) -> p h n", h=hc),
                                       ACT.Exp).then_inc(exp_sb.sem, 1)

                def turned(s):
                    l, c, k, cols = step(s)
                    if own and l:
                        act.wait_ge(hn_ps.sem, hn_ps.after(t, k - CHAINS))
                        act.wait_ge(agg_ps.sem, agg_ps.after(t, k - CHAINS))
                        act.activation(hn16[:, :, c * CG:(c + 1) * CG], ps_t16[:, 0:2 * CW].rearrange(
                            "p (a g n) -> p a g n", a=2, g=CG), ACT.Copy).then_inc(hn_sb.sem, 1)

                def candidate(s):
                    l, c, k, cols = step(s)
                    if own:
                        act.wait_ge(pre_sb.sem, pre_sb.after(t, k))
                        act.wait_ge(h_sb.sem, h_sb.after(t, k - CHAINS))
                        act.activation(cand[:, cols], pre[:, cols], ACT.Tanh, bias=b_ih[:, 2:3]).then_inc(cand_sb.sem, 1)

                def hidden_half(s):
                    l, c, k, cols = step(s)
                    if own:
                        act.wait_ge(hh_ps.sem, hh_ps.after(t, k))
                        act.wait_ge(pre_sb.sem, pre_sb.after(t, k - CHAINS))
                        act.activation(h_half[:, cols], hi[c][:, 0:CW], ACT.Identity, scale=half_unscale[:],
                                       bias=b_half[:, 2:3]).then_inc(half_sb.sem, 1)

                def sums_high(s):
                    l, c, k, cols = step(s)
                    if own:
                        act.wait_ge(agg_ps.sem, agg_ps.after(t, k))
                        act.wait_ge(i_ps.sem, i_ps.after(t, k - CHAINS))
                        act.activation(agg16[:, 0, cols], ps_t[:, 0:CW], ACT.Copy,
                                       scale=AGG_SCALE / H_SCALE).then_inc(agghi_sb.sem, 1)

                def state_high(s):
                    l, c, k, cols = step(s)
                    if own and l + 1 < layers:
                        act.wait_ge(h_sb.sem, h_sb.after(t, k))
                        act.activation(h16[:, 0, cols], hT[lane][:, cols], ACT.Copy,
                                       scale=H_SCALE / 2).then_inc(hhi_sb.sem, 1)

                def reset_gate(s):
                    l, c, k, cols = step(s)
                    if own:
                        act.wait_ge(rz_ps.sem, rz_ps.after(t, k))
                        act.wait_ge(gated_sb.sem, gated_sb.after(t, k - CHAINS))
                        act.activation(t_r[:, cols], rz[c][:, 0:CW], ACT.Tanh, scale=half_unscale[:],
                                       bias=b_half[:, 0:1]).then_inc(r_sb.sem, 1)

                def update_gate(s):
                    l, c, k, cols = step(s)
                    if own:
                        act.wait_ge(rz_ps.sem, rz_ps.after(t, k))
                        act.wait_ge(new_sb.sem, new_sb.after(t, k - CHAINS))
                        act.activation(t_z[:, cols], rz[c][:, CW:2 * CW], ACT.Tanh, scale=half_unscale[:],
                                       bias=b_half[:, 1:2]).then_inc(z_sb.sem, 1)

                def normed(grp, n, dst, half):
                    if n == 0 and head or n and tail:
                        act.wait_ge(shift_sb[n].sem, shift_sb[n].after(grp))
                        i = min(n, 1)
                        for g in range(half * G // 2, (half + 1) * G // 2):
                            act.activation(dst[:, g], t_ln[i][:, g], ACT.Identity, scale=rstd[i][:, g:g + 1],
                                           bias=shift[i][:, g:g + 1]).then_inc(ln_sb[n].sem, 1)

                def first_part(i):
                    if ahead:
                        for x in stacked:
                            act.wait_ge(x.sem, x.after(nxt, heads))
                        copy_out(parts[i][:, 0], slot["qk", i][:], qk_ps[i], far, part1[i])

                def first_high(c):
                    if head:
                        gs, cols = slice(c * CG, (c + 1) * CG), slice(c * CW, (c + 1) * CW)
                        act.wait_ge(agg_ps.sem, agg_ps.after(t, steps))
                        act.activation(hn16[:, 0, gs], x1[other][:, gs], ACT.Copy, scale=H_SCALE).then_inc(nhi_sb.sem, 1)
                        act.wait_ge(h0_sb.sem, h0_sb.after(nxt))
                        act.activation(h16[:, 0, cols], hT[other][:, cols], ACT.Copy,
                                       scale=H_SCALE / 2).then_inc(hhi_sb.sem, 1)

                sums_high(0)
                if ahead:
                    copy_out(xT[:], slot["xT"][:], xT_ps, far, xT_sb)
                if head:
                    act.wait_ge(adj2_sb.sem, adj2_sb.after(last))
                    act.wait_ge(adj3_sb.sem, adj3_sb.after(last))
                    copy_out(adjT[other][:], slot["adjT"][:].rearrange("p (g n) -> p g n", g=G),
                             adjT_ps, nxt, adjT_sb)
                sums_high(1)
                hidden_half(0)
                update_gate(0)
                reset_gate(0)
                hidden_half(1)
                reset_gate(1)
                first_part(0)
                update_gate(1)
                candidate(0)
                state_high(0)
                first_part(1)
                candidate(1)
                normed(last, 1, x2, 0)
                turned(2)
                state_high(1)
                exps(0)
                sums_high(2)
                exps(1)
                normed(last, 1, x2, 1)
                turned(3)
                hidden_half(2)
                if tail:
                    copy_out(x2T[:], slot["x2T"][:], x2T_ps, last, x2T_sb)
                reset_gate(2)
                exps(2)
                hidden_half(3)
                sums_high(3)
                candidate(2)
                update_gate(2)
                if tail:
                    copy_out(h2[:], slot["h2"][:].rearrange("p (g n) -> p g n", g=G), h2_ps, last, h2_sb)
                reset_gate(3)
                exps(3)
                state_high(2)
                update_gate(3)
                if ahead:
                    copy_out(parts[0][:, 3], rest[0][:], rest1[0], far, part2[0])
                candidate(3)
                turned(4)
                if ahead:
                    copy_out(parts[1][:, 1], rest[1][:], rest1[1], far, part2[1])
                sums_high(4)
                state_high(3)
                hidden_half(4)
                exps(4)
                reset_gate(4)
                turned(5)
                exps(5)
                update_gate(4)
                candidate(4)
                sums_high(5)
                hidden_half(5)
                normed(last, 2, x3, 0)
                state_high(4)
                exps(6)
                reset_gate(5)
                normed(last, 2, x3, 1)
                hidden_half(6)
                turned(6)
                update_gate(5)
                if tail:
                    copy_out(hsT[:], slot["hs"][:], hs_ps, last, hs_sb)
                sums_high(6)
                exps(7)
                candidate(5)
                state_high(5)
                if tail:
                    copy_out(hid[:, 0], slot["hid", 0][:], hid_ps, last, hid_sb, 1, b31[:, 0:1], ACT.Relu)
                update_gate(6)
                reset_gate(6)
                turned(7)
                candidate(6)
                if head:
                    copy_out(oT[:], slot["oT"][:], oT_ps, nxt, oT_sb)
                sums_high(7)
                if ahead:
                    act.wait_ge(o_ps.sem, o_ps.after(t, G))
                    copy_out(v1[lane][:, :, :, 0:dh], slot["v"][:].rearrange("p (g h d) -> p g h d", g=G, d=dh),
                             v_ps, far, v_sb)
                hidden_half(7)
                state_high(6)
                reset_gate(7)
                update_gate(7)
                if tail:
                    copy_out(hid[:, 1], slot["hid", 1][:], hid_ps, last, hid_sb, 2, b31[:, 1:2], ACT.Relu)
                turned(8)
                candidate(7)
                sums_high(8)
                state_high(7)
                hidden_half(8)
                normed(nxt, 0, x1[other], 0)
                turned(9)
                reset_gate(8)
                sums_high(9)
                update_gate(8)
                hidden_half(9)
                state_high(8)
                normed(nxt, 0, x1[other], 1)
                reset_gate(9)
                update_gate(9)
                if head:
                    act.wait_ge(hT_ps.sem, hT_ps.after(last))
                    act.wait_ge(h0_ps.sem, h0_ps.after(nxt))
                    act.activation(hT[other][:], slot["h0"][:], ACT.Copy, scale=2.0).then_inc(h0_sb.sem, 1)
                first_high(0)
                candidate(8)
                candidate(9)
                first_high(1)

            halves(act, half)

        @block.vector
        def _(dve):
            dve.wait_ge(s_const, 16 * len(loads))
            dve.tensor_scalar(wq[:], wq[:], float(dh) ** -0.5, None, ALU.mult).then_inc(s_dve0, 1)
            dve.tensor_scalar(nodemask[:], nodemask[:], 0.5, None, ALU.mult)
            dve.tensor_tensor(b_half[:, 0:2], b_ih[:, 0:2], b_hh[:, 0:2], ALU.add).then_inc(s_dve0, 1)
            dve.tensor_scalar(b_half[:, 2:3], b_hh[:, 2:3], 0.5, None, ALU.mult).then_inc(s_dve0, 1)
            dve.tensor_scalar(eps3[:], eps3[:], 1.0, None, ALU.add).then_inc(s_dve0, 1)
            dve.wait_ge(s_dve0, 4)
            dve.tensor_scalar(b_half[:, 0:2], b_half[:, 0:2], 0.5, None, ALU.mult).then_inc(s_dve0, 1)
            dve.wait_ge(s_pool0, 11)
            dve.tensor_copy(ident16[:], ident[:]).then_inc(s_dve0, 1)
            dve.tensor_scalar(eps_ident[:], ident[:], eps3[:, 0:1], None, ALU.mult).then_inc(s_dve0, 1)
            for l in range(layers):
                dve.wait_ge(s_pe0, l + 1)
                dve.tensor_copy(w_in[:, l], bank[l % 2][:, 0:3 * P]).then_inc(s_dve0, 1)
            dve.wait_ge(s_dve0, 7 + layers)
            all_in = w_in[:].rearrange("p l n -> p (l n)")
            for i, w in enumerate((w_hh[:], all_in)):
                dve.tensor_reduce(extremes[:, i:i + 1], w, AX_X, ALU.max)
                ins = dve.tensor_reduce(extremes[:, 2 + i:3 + i], w, AX_X, ALU.min)
            chain = signal_chain(dve, ctx.enter_context(nc.semaphore("dve_weights")))
            chain(ins)
            chain(dve.tensor_scalar(extremes[:, 2:4], extremes[:, 2:4], -1.0, None, ALU.mult))
            dve.tensor_reduce(w_rec[:], extremes[:], AX_X, ALU.max).then_inc(s_dve0, 1)
            dve.wait_ge(s_pool0, 12)
            chain(dve.tensor_scalar(w_max[:], w_max[:], 1e-30, None, ALU.max))
            chain(dve.tensor_scalar(w_pow[:].bitcast(I32), w_max[:].bitcast(I32), 0x7F800000, None, ALU.bitwise_and))
            chain(dve.reciprocal(w_rec[:], w_pow[:]))
            dve.tensor_scalar(s_hh[:], w_rec[:], W_TOP, None, ALU.mult)
            dve.tensor_scalar(s_in[:], w_rec[:], W_TOP * H_SCALE / AGG_SCALE, None, ALU.mult)
            dve.tensor_scalar(unscale[:], w_pow[:], 1.0 / (W_TOP * H_SCALE), None, ALU.mult)
            chain(dve.tensor_scalar(half_unscale[:], w_pow[:], 0.5 / (W_TOP * H_SCALE), None, ALU.mult))
            high_in, low_in = (w_in16[:, c].rearrange("p l n -> p (l n)") for c in range(2))
            dve.tensor_scalar(w_hh16[:, 0], w_hh[:], s_hh[:], None, ALU.mult)
            chain(dve.tensor_scalar(high_in, all_in, s_in[:], None, ALU.mult))
            dve.scalar_tensor_tensor(w_hh16[:, 1], w_hh[:], s_hh[:], w_hh16[:, 0], ALU.mult, ALU.subtract)
            chain(dve.scalar_tensor_tensor(low_in, all_in, s_in[:], high_in, ALU.mult, ALU.subtract))
            dve.sem_inc(s_start, 1)

            def half(t, lane, ahead, head, own, tail):
                far, nxt, last, other = t.plus(2), t.plus(1), t.plus(-1), 1 - lane
                slot = banks_of()

                def split(grp, ln, k, cols):
                    dve.wait_ge(hhi_sb.sem, hhi_sb.after(grp, k))
                    dve.scalar_tensor_tensor(h16[:, 1, cols], hT[ln][:, cols], H_SCALE / 2, h16[:, 0, cols], ALU.mult,
                                             ALU.subtract).then_inc(hlo_sb.sem, 1)

                def first_state(c):
                    if head:
                        l, c, k, cols = step(c)
                        gs = slice(c * CG, (c + 1) * CG)
                        dve.wait_ge(nhi_sb.sem, nhi_sb.after(nxt, c + 1))
                        dve.scalar_tensor_tensor(hn16[:, 1, gs], x1[other][:, gs], H_SCALE, hn16[:, 0, gs], ALU.mult,
                                                 ALU.subtract).then_inc(nlo_sb.sem, 1)
                        split(nxt, other, k, cols)

                def norm_stats(grp, n):
                    if tail if n else head:
                        i = min(n, 1)
                        dve.wait_ge(t_sb[n].sem, t_sb[n].after(grp))
                        for g in range(G):
                            ins = dve.bn_stats(stats[i][:, g], t_ln[i][:, g])
                        ins.then_inc(stats_sb[n].sem, 1)

                def norm_moments(grp, n):
                    if tail if n else head:
                        i = min(n, 1)
                        dve.wait_ge(s_const, 16)
                        dve.wait_ge(stats_sb[n].sem, stats_sb[n].after(grp))
                        for g in range(G):
                            ins = dve.bn_aggr(mean_var[i][:, g], stats[i][:, g])
                        ins.then_inc(var_sb[n].sem, 1)

                def low(s):
                    l, c, k, cols = step(s)
                    if own:
                        dve.wait_ge(agghi_sb.sem, agghi_sb.after(t, k))
                        dve.scalar_tensor_tensor(agg16[:, 1, cols], ps_t[:, 0:CW], AGG_SCALE / H_SCALE,
                                                 agg16[:, 0, cols], ALU.mult, ALU.subtract).then_inc(agglo_sb.sem, 1)

                def gated(s):
                    l, c, k, cols = step(s)
                    if own:
                        dve.wait_ge(half_sb.sem, half_sb.after(t, k))
                        dve.wait_ge(r_sb.sem, r_sb.after(t, k))
                        dve.scalar_tensor_tensor(h_half[:, cols], t_r[:, cols], 1.0, h_half[:, cols], ALU.add,
                                                 ALU.mult).then_inc(gated_sb.sem, 1)

                def old_state(s):
                    l, c, k, cols = step(s)
                    if own:
                        dve.wait_ge(z_sb.sem, z_sb.after(t, k))
                        dve.scalar_tensor_tensor(kept[:, cols], t_z[:, cols], 1.0, hT[lane][:, cols], ALU.add,
                                                 ALU.mult).then_inc(kept_sb.sem, 1)

                def before_tanh(s):
                    l, c, k, cols = step(s)
                    if own:
                        dve.wait_ge(gated_sb.sem, gated_sb.after(t, k))
                        dve.wait_ge(i_ps.sem, i_ps.after(t, k))
                        dve.scalar_tensor_tensor(pre[:, cols], hi[c][:, CW:2 * CW], unscale[:], h_half[:, cols],
                                                 ALU.mult, ALU.add).then_inc(pre_sb.sem, 1)

                def renew(s):
                    l, c, k, cols = step(s)
                    if own:
                        dve.wait_ge(z_sb.sem, z_sb.after(t, k))
                        dve.wait_ge(cand_sb.sem, cand_sb.after(t, k))
                        dve.scalar_tensor_tensor(renewed[:, cols], t_z[:, cols], 1.0, cand[:, cols], ALU.subtract,
                                                 ALU.mult).then_inc(new_sb.sem, 1)

                def new_state(s):
                    l, c, k, cols = step(s)
                    if own:
                        dve.wait_ge(kept_sb.sem, kept_sb.after(t, k))
                        dve.wait_ge(new_sb.sem, new_sb.after(t, k))
                        dve.scalar_tensor_tensor(hT[lane][:, cols], kept[:, cols], 0.5, renewed[:, cols], ALU.mult,
                                                 ALU.subtract).then_inc(h_sb.sem, 1)

                def state_low(s):
                    l, c, k, cols = step(s)
                    if own and l + 1 < layers:
                        split(t, lane, k + CHAINS, cols)

                def maxes(grp, i):
                    if head if grp is nxt else ahead:
                        c, g = i // G, i % G
                        if i == 0:
                            dve.wait_ge(m_ps.sem, m_ps.after(nxt))
                        dve.wait_ge(s_ps.sem, s_ps.after(grp, i + 1))
                        dve.tensor_reduce(maxima[:, c * hc:(c + 1) * hc, g],
                                          slot["s", i][:].rearrange("p (h n) -> p h n", h=hc), AX_X,
                                          ALU.max).then_inc(max_sb.sem, 1)

                def probs(i):
                    if head:
                        c, g = i % 2, i // 2
                        dve.wait_ge(exp_sb.sem, exp_sb.after(nxt, i + 1))
                        ev = e[g % 2][:, c * hc:(c + 1) * hc]
                        dve.scalar_tensor_tensor(ev, adjT[other][:, g].unsqueeze(1).to_broadcast([P, hc, P]),
                                                 ADJ_EPS, ev, ALU.add, ALU.mult).then_inc(prob_sb.sem, 1)

                def sums_inverse(g):
                    if head:
                        o = slot["o", g][:, 0:heads * vw].rearrange("p (h w) -> p h w", w=vw)
                        dve.wait_ge(o_ps.sem, o_ps.after(nxt, g + 1))
                        dve.reciprocal(r_sum[g % 2][:], o[:, :, dh]).then_inc(rsum_sb.sem, 1)

                def normalise(g):
                    if head:
                        o = slot["o", g][:, 0:heads * vw].rearrange("p (h w) -> p h w", w=vw)
                        dve.wait_ge(rsum_sb.sem, rsum_sb.after(nxt, g + 1))
                        dve.tensor_tensor(o_n[:, g], o[:, :, 0:dh],
                                          r_sum[g % 2][:].unsqueeze(2).to_broadcast([P, heads, dh]),
                                          ALU.mult).then_inc(norm_sb.sem, 1)

                def second_rest(i):
                    if ahead:
                        dve.wait_ge(part1[i].sem, part1[i].after(far))
                        dve.tensor_tensor(rest[i][:], slot["qk", i][:], parts[i][:, 0],
                                          ALU.subtract).then_inc(rest1[i].sem, 1)

                low(0)
                maxes(nxt, 5)
                maxes(nxt, 6)
                if tail:
                    dve.wait_ge(ln_sb[3].sem, ln_sb[3].after(last.plus(-1), G))
                    dve.wait_ge(hT_ps.sem, hT_ps.after(last))
                    for g in range(G):
                        b = last.times(G, g)
                        ins = dve.scalar_tensor_tensor(
                            t_ln[1][:, g], slot["hT"][:, g * P:(g + 1) * P], nodemask[:, bass.ds(b, 1)],
                            x1[other][:, g], ALU.mult, ALU.add)
                    ins.then_inc(t_sb[1].sem, 1)
                low(1)
                gated(0)
                maxes(nxt, 7)
                old_state(0)
                before_tanh(0)
                norm_stats(last, 1)
                if head:
                    dve.wait_ge(m_ps.sem, m_ps.after(nxt))
                    dve.wait_ge(m_stacked.sem, m_stacked.after(t, 3))
                    mT = slot["m"][0:heads * G, 0:P]
                    dve.tensor_copy(m_parts[:, 0], mT).then_inc(m1_sb.sem, 1)
                    dve.wait_ge(m1_sb.sem, m1_sb.after(nxt))
                    dve.tensor_tensor(m_rest[:], mT, m_parts[:, 0], ALU.subtract).then_inc(mr_sb.sem, 1)
                    dve.wait_ge(mr_sb.sem, mr_sb.after(nxt))
                    dve.tensor_copy(m_parts[:, 1], m_rest[:]).then_inc(m2_sb.sem, 1)
                    dve.wait_ge(m2_sb.sem, m2_sb.after(nxt))
                    dve.tensor_tensor(m_parts[:, 2], m_rest[:], m_parts[:, 1], ALU.subtract).then_inc(m3_sb.sem, 1)
                norm_moments(last, 1)
                gated(1)
                renew(0)
                new_state(0)
                before_tanh(1)
                state_low(0)
                second_rest(0)
                renew(1)
                old_state(1)
                new_state(1)
                second_rest(1)
                state_low(1)
                low(2)
                probs(0)
                gated(2)
                before_tanh(2)
                probs(1)
                low(3)
                probs(2)
                old_state(2)
                renew(2)
                new_state(2)
                gated(3)
                probs(3)
                before_tanh(3)
                state_low(2)
                old_state(3)
                if tail:
                    dve.wait_ge(ln_sb[1].sem, ln_sb[1].after(last, G))
                    dve.wait_ge(d2_ps.sem, d2_ps.after(last))
                    for g in range(G):
                        ins = dve.scalar_tensor_tensor(t_ln[1][:, g], slot["d2"][:, g * P:(g + 1) * P],
                                                       dis[other][:, g:g + 1], x2[:, g], ALU.mult, ALU.add)
                    ins.then_inc(t_sb[2].sem, 1)
                renew(3)
                new_state(3)
                low(4)
                sums_inverse(0)
                state_low(3)
                normalise(0)
                norm_stats(last, 2)
                norm_moments(last, 2)
                gated(4)
                before_tanh(4)
                probs(4)
                old_state(4)
                renew(4)
                low(5)
                new_state(4)
                state_low(4)
                if ahead:
                    dve.tensor_copy(parts[0][:, 1:3], parts[0][:, 0:1].to_broadcast([P, 2, W]))
                    dve.wait_ge(part2[0].sem, part2[0].after(far))
                    dve.tensor_copy(parts[0][:, 4], parts[0][:, 3]).then_inc(copies[0].sem, 1)
                sums_inverse(1)
                gated(5)
                if head:
                    dve.wait_ge(adj_loaded.sem, adj_loaded.after(nxt))
                    dve.wait_ge(agg_ps.sem, agg_ps.after(last, steps))
                    dve.tensor_scalar(adj_on[other][:], adj[:], 0.0, None, ALU.not_equal).then_inc(adj_on_sb.sem, 1)
                probs(5)
                normalise(1)
                before_tanh(5)
                probs(6)
                old_state(5)
                low(6)
                if ahead:
                    dve.tensor_copy(parts[1][:, 5], parts[1][:, 0])
                    dve.wait_ge(part2[1].sem, part2[1].after(far))
                    dve.tensor_copy(parts[1][:, 3:5], parts[1][:, 0:2]).then_inc(copies[1].sem, 1)
                renew(5)
                probs(7)
                new_state(5)
                sums_inverse(2)
                normalise(2)
                state_low(5)
                sums_inverse(3)
                gated(6)
                normalise(3)
                before_tanh(6)
                old_state(6)
                if head:
                    dve.wait_ge(off_sb.sem, off_sb.after(nxt))
                    dve.wait_ge(dis_sb.sem, dis_sb.after(t))
                    dve.reduce_sum(deg[:], adj_off[:], AX_X).then_inc(deg_sb.sem, 1)
                renew(6)
                low(7)
                new_state(6)
                if head:
                    dve.wait_ge(ln_sb[0].sem, ln_sb[0].after(t, G))
                    dve.wait_ge(y_ps.sem, y_ps.after(nxt))
                    dve.wait_ge(res0_sb.sem, res0_sb.after(nxt))
                    dve.tensor_tensor(t_ln[0][:], slot["y"][:].rearrange("p (g n) -> p g n", g=G), res0[other][:],
                                      ALU.add).then_inc(t_sb[0].sem, 1)
                state_low(6)
                norm_stats(nxt, 0)
                gated(7)
                norm_moments(nxt, 0)
                before_tanh(7)
                old_state(7)
                maxes(far, 0)
                renew(7)
                new_state(7)
                maxes(far, 1)
                low(8)
                state_low(7)
                maxes(far, 2)
                if tail:
                    dve.wait_ge(ln_sb[2].sem, ln_sb[2].after(last, G))
                    dve.wait_ge(y3_ps.sem, y3_ps.after(last))
                    dve.wait_ge(res3_sb.sem, res3_sb.after(last))
                    dve.tensor_tensor(t_ln[1][:], slot["y3"][:].rearrange("p (g n) -> p g n", g=G), res3[:],
                                      ALU.add).then_inc(t_sb[3].sem, 1)
                norm_stats(last, 3)
                gated(8)
                low(9)
                maxes(far, 3)
                norm_moments(last, 3)
                before_tanh(8)
                old_state(8)
                maxes(far, 4)
                gated(9)
                old_state(9)
                before_tanh(9)
                first_state(0)
                renew(8)
                renew(9)
                new_state(8)
                new_state(9)
                first_state(1)

            halves(dve, half)

        @block.tensor
        def _(pe):
            pe.wait_ge(s_const, 16 * len(loads))
            for l in range(layers):
                if l >= 2:
                    pe.wait_ge(s_dve0, 7 + l - 1)
                pe.matmul(bank[l % 2][:, 0:3 * P], w_l[:, l], w_ih[:], start=True, stop=True).then_inc(s_pe0, 1)
            pe.wait_ge(s_start, 1)

            def turn(dst, src, done, idn=ident):
                for g in range(G):
                    ins = pe.transpose(dst[:, g * P:(g + 1) * P], src[:, g * P:(g + 1) * P], idn[:])
                ins.then_inc(done.sem, 1)

            def flat(a):
                return a[:].rearrange("p g n -> p (g n)")

            def per_graph(dst, lhs, rhs, done):
                for g in range(G):
                    ins = pe.matmul(dst[:, g * P:(g + 1) * P], lhs(g), rhs(g), start=True, stop=True)
                ins.then_inc(done.sem, 1)

            def blk(a):
                return lambda g: a[:, g * P:(g + 1) * P]

            def row(a):
                return lambda g: a[:, g]

            def half(t, lane, ahead, head, own, tail):
                far, nxt, last, other = t.plus(2), t.plus(1), t.plus(-1), 1 - lane
                runs = {2: ahead, 1: head, 0: own, -1: tail}
                after_full_half = t.a or 1 < t.b <= groups - 2

                def take(name):
                    n = next(i for i, p in enumerate(pieces) if p[0] == name)
                    assert runs[pieces[n][1]]
                    m = n - len(ring)
                    while m >= 0 and not runs[pieces[m][1]]:
                        m -= len(ring)
                    if m >= 0:
                        _, off, read, k = pieces[m]
                        pe.wait_ge(read.sem, read.after(t.plus(off), k))
                    elif after_full_half:
                        m = max(i for i in range(len(pieces)) if i % len(ring) == n % len(ring))
                        _, off, read, k = pieces[m]
                        pe.wait_ge(read.sem, read.after(t.plus(off - 1), k))
                    return ring[n % len(ring)]

                def leave():
                    for b in range(len(ring)):
                        used = [p for i, p in enumerate(pieces) if i % len(ring) == b and runs[p[1]]]
                        if used:
                            _, off, read, k = used[-1]
                            pe.wait_ge(read.sem, read.after(t.plus(off), k))

                def scores(name, i, ln, c, g, a, b, rows, done):
                    dst = take((name, i))
                    for j in range(hc):
                        ins = pe.matmul(dst[:, j * P:(j + 1) * P],
                                        stack[a][0:rows, ln, c * hc + j, g * P:(g + 1) * P],
                                        stack[b][0:rows, ln, c * hc + j, g * P:(g + 1) * P], start=True, stop=True)
                    ins.then_inc(done.sem, 1)

                def query_rows(grp, ln, i):
                    if head if grp is nxt else ahead:
                        c, g = i // G, i % G
                        if g == 0:
                            pe.wait_ge(stacked[c].sem, stacked[c].after(grp, heads))
                        scores("s", i, ln, c, g, 0, 1, KS, s_ps)

                def key_rows(i):
                    if head:
                        if i == 0:
                            pe.wait_ge(m_stacked.sem, m_stacked.after(nxt, 3))
                        scores("st", i, other, i % 2, i // 2, 1, 0, KS + 3, st_ps)

                def attend(g):
                    if head:
                        dst = take(("o", g))
                        pe.wait_ge(prob_sb.sem, prob_sb.after(nxt, 2 * g + 2))
                        for h in range(heads):
                            ins = pe.matmul(dst[:, h * vw:(h + 1) * vw], e[g % 2][:, h], v1[other][:, g, h],
                                            start=True, stop=True)
                        ins.then_inc(o_ps.sem, 1)

                def gate_parts(dst, w, gate, x, start, stop):
                    cols = slice(gate * P, (gate + 1) * P)
                    for n, (a, b) in enumerate(((0, 0), (0, 1), (1, 0))):
                        ins = pe.matmul(dst, w(a)[:, cols], x(b), start=(start and n == 0), stop=(stop and n == 2))
                    return ins

                def turn_state(s):
                    l, c, k, cols = step(s)
                    if own and l:
                        pe.wait_ge(hlo_sb.sem, hlo_sb.after(t, k))
                        pe.wait_ge(agglo_sb.sem, agglo_sb.after(t, k - 1))
                        for a in range(2):
                            for g in range(CG):
                                n = a * CG + g
                                ins = pe.transpose(ps_t16[:, n * P:(n + 1) * P],
                                                   h16[:, a, (c * CG + g) * P:(c * CG + g + 1) * P], ident16[:])
                        ins.then_inc(hn_ps.sem, 1)

                def hidden_gates(s):
                    l, c, k, cols = step(s)
                    if own:
                        pe.wait_ge(hlo_sb.sem, hlo_sb.after(t, k))
                        pe.wait_ge(r_sb.sem, r_sb.after(t, k - CHAINS))
                        pe.wait_ge(z_sb.sem, z_sb.after(t, k - CHAINS))
                        w, x = (lambda a: w_hh16[:, a]), (lambda b: h16[:, b, cols])
                        gate_parts(rz[c][:, 0:CW], w, 0, x, True, False)
                        gate_parts(rz[c][:, CW:2 * CW], w, 1, x, False, False)

                def hidden_n(s):
                    l, c, k, cols = step(s)
                    if own:
                        pe.wait_ge(hlo_sb.sem, hlo_sb.after(t, k))
                        pe.wait_ge(pre_sb.sem, pre_sb.after(t, k - CHAINS))
                        gate_parts(hi[c][:, 0:CW], lambda a: w_hh16[:, a], 2, lambda b: h16[:, b, cols],
                                   True, True).then_inc(hh_ps.sem, 1)

                def neighbours(s):
                    l, c, k, cols = step(s)
                    if own:
                        if l:
                            pe.wait_ge(hn_sb.sem, hn_sb.after(t, k - CHAINS))
                        else:
                            pe.wait_ge(adj_on_sb.sem, adj_on_sb.after(t))
                            pe.wait_ge(nlo_sb.sem, nlo_sb.after(t, k))
                            pe.wait_ge(agglo_sb.sem, agglo_sb.after(t, k - 1))
                        for g in range(CG):
                            for a in range(2):
                                ins = pe.matmul(ps_t[:, g * P:(g + 1) * P], hn16[:, a, c * CG + g],
                                                adj_on[lane][:, c * CG + g], start=(a == 0), stop=(a == 1))
                        ins.then_inc(agg_ps.sem, 1)

                def input_gates(s):
                    l, c, k, cols = step(s)
                    if own:
                        pe.wait_ge(agglo_sb.sem, agglo_sb.after(t, k))
                        w, x = (lambda a: w_in16[:, a, l]), (lambda b: agg16[:, b, cols])
                        gate_parts(rz[c][:, 0:CW], w, 0, x, False, False)
                        gate_parts(rz[c][:, CW:2 * CW], w, 1, x, False, True).then_inc(rz_ps.sem, 1)

                def input_n(s):
                    l, c, k, cols = step(s)
                    if own:
                        pe.wait_ge(agglo_sb.sem, agglo_sb.after(t, k))
                        pe.wait_ge(half_sb.sem, half_sb.after(t, k))
                        gate_parts(hi[c][:, CW:2 * CW], lambda a: w_in16[:, a, l], 2, lambda b: agg16[:, b, cols],
                                   True, True).then_inc(i_ps.sem, 1)

                def project(i):
                    if ahead:
                        dst = take(("qk", i))
                        pe.wait_ge(xT_sb.sem, xT_sb.after(far))
                        pe.matmul(dst[:], (wq, wk)[i][:], xT[:], start=True, stop=True).then_inc(qk_ps[i].sem, 1)

                def first_dense(h):
                    if tail:
                        b = take(("hid", h))
                        pe.wait_ge(hs_sb.sem, hs_sb.after(last))
                        pe.matmul(b[:], w31[:, h * P:(h + 1) * P], hsT[:], start=True, stop=True).then_inc(hid_ps.sem, 1)

                if ahead:
                    b = take("xT")
                    pe.wait_ge(x_loaded.sem, x_loaded.after(far))
                    turn(b, flat(x_in), xT_ps)
                neighbours(0)
                if head:
                    b = take("adjT")
                    pe.wait_ge(adj_loaded.sem, adj_loaded.after(nxt))
                    turn(b, flat(adj), adjT_ps)
                hidden_n(0)
                query_rows(nxt, other, 5)
                hidden_gates(0)
                if tail:
                    b = take("hT")
                    pe.wait_ge(h_sb.sem, h_sb.after(last, steps))
                    turn(b, hT[other], hT_ps)
                query_rows(nxt, other, 6)
                neighbours(1)
                input_gates(0)
                query_rows(nxt, other, 7)
                hidden_gates(1)
                input_n(0)
                input_gates(1)
                hidden_n(1)
                if head:
                    b = take("m")
                    pe.wait_ge(max_sb.sem, max_sb.after(nxt, 2 * G))
                    pe.transpose(b[0:heads * G, 0:P], maxima[:].rearrange("p h g -> p (h g)"),
                                 ident[:]).then_inc(m_ps.sem, 1)
                project(0)
                input_n(1)
                project(1)
                turn_state(2)
                hidden_gates(2)
                hidden_n(2)
                key_rows(0)
                neighbours(2)
                key_rows(1)
                turn_state(3)
                input_gates(2)
                if tail:
                    b = take("x2T")
                    pe.wait_ge(ln_sb[1].sem, ln_sb[1].after(last, G))
                    turn(b, flat(x2), x2T_ps)
                neighbours(3)
                key_rows(2)
                input_n(2)
                hidden_n(3)
                hidden_gates(3)
                if tail:
                    b = take("h2")
                    pe.matmul(b[:].rearrange("p (g n) -> p g n", g=G), ones[:],
                              b2g[0:1].unsqueeze(1).to_broadcast([1, G, P]), start=True, stop=False)
                    pe.wait_ge(x2T_sb.sem, x2T_sb.after(last))
                    for g in range(G):
                        ins = pe.matmul(b[:, g * P:(g + 1) * P], x2T[:, g * P:(g + 1) * P], w2g[:], start=False,
                                        stop=(g == G - 1))
                    ins.then_inc(h2_ps.sem, 1)
                input_gates(3)
                key_rows(3)
                if tail:
                    b = take("d2")
                    pe.wait_ge(h2_sb.sem, h2_sb.after(last))
                    pe.wait_ge(adj2_sb.sem, adj2_sb.after(last))
                    per_graph(b, row(adj2[other]), row(h2), d2_ps)
                input_n(3)
                attend(0)
                turn_state(4)
                key_rows(4)
                neighbours(4)
                hidden_gates(4)
                hidden_n(4)
                key_rows(5)
                input_gates(4)
                turn_state(5)
                input_n(4)
                key_rows(6)
                hidden_n(5)
                hidden_gates(5)
                neighbours(5)
                attend(1)
                input_gates(5)
                key_rows(7)
                input_n(5)
                hidden_n(6)
                hidden_gates(6)
                turn_state(6)
                if tail:
                    b = take("hs")
                    pe.wait_ge(ln_sb[2].sem, ln_sb[2].after(last, G))
                    pe.wait_ge(adj3_sb.sem, adj3_sb.after(last))
                    per_graph(b, row(x3), row(adj3[other]), hs_ps)
                neighbours(6)
                attend(2)
                first_dense(0)
                input_n(6)
                input_gates(6)
                attend(3)
                hidden_n(7)
                turn_state(7)
                hidden_gates(7)
                if head:
                    b = take("oT")
                    pe.wait_ge(norm_sb.sem, norm_sb.after(nxt, G))
                    turn(b, o_n[:].rearrange("p g h d -> p (g h d)"), oT_ps)
                neighbours(7)
                if ahead:
                    b = take("v")
                    pe.wait_ge(xT_sb.sem, xT_sb.after(far))
                    per_graph(b, blk(xT), lambda g: wv[:], v_ps)
                if head:
                    b = take("y")
                    pe.wait_ge(oT_sb.sem, oT_sb.after(nxt))
                    per_graph(b, blk(oT), lambda g: wo[:], y_ps)
                input_gates(7)
                input_n(7)
                first_dense(1)
                query_rows(far, lane, 0)
                query_rows(far, lane, 1)
                turn_state(8)
                hidden_gates(8)
                hidden_n(8)
                neighbours(8)
                if tail:
                    b = take("y3")
                    pe.wait_ge(hid_sb.sem, hid_sb.after(last, 2))
                    for g in range(G):
                        for h in range(2):
                            ins = pe.matmul(b[:, g * P:(g + 1) * P], hid[:, h, g * P:(g + 1) * P], w32[:, h],
                                            start=(h == 0), stop=(h == 1))
                    ins.then_inc(y3_ps.sem, 1)
                query_rows(far, lane, 2)
                input_gates(8)
                turn_state(9)
                query_rows(far, lane, 3)
                input_n(8)
                neighbours(9)
                query_rows(far, lane, 4)
                hidden_n(9)
                hidden_gates(9)
                input_gates(9)
                input_n(9)
                if head:
                    b = take("h0")
                    pe.wait_ge(ln_sb[0].sem, ln_sb[0].after(nxt, G))
                    turn(b, flat(x1[other]), h0_ps)
                if not (ahead and head and own and tail):
                    leave()

            halves(pe, half)


def signal_chain(engine, sem):
    done = [0]

    def link(ins):
        done[0] += 1
        ins.then_inc(sem, 1)
        engine.wait_ge(sem, done[0])

    return link


def kernel(**inputs):
    import numpy as np
    import concourse.bacc as bacc
    from concourse.bass_utils import run_bass_kernel_spmd

    a = {n: np.asarray(v) for n, v in inputs.items()}
    lay = {
        "x": a["x"], "adj": a["adj"], "nodemask_T": a["nodemask"].T,
        "L0_Wq_T": a["L0_gnn_Wq"].T, "L0_Wk_T": a["L0_gnn_Wk"].T, "L0_Wv_T": a["L0_gnn_Wv"].T,
        "L0_Wo_T": a["L0_gnn_Wo"].T, "L0_bo": a["L0_gnn_bo"].reshape(1, -1),
        "L1_weight_T": a["L1_gnn_weight"].transpose(0, 2, 1),
        "L1_w_ih_T": a["L1_gnn_w_ih"].T, "L1_w_hh_T": a["L1_gnn_w_hh"].T,
        "L1_b_ih": a["L1_gnn_b_ih"].reshape(3, -1).T, "L1_b_hh": a["L1_gnn_b_hh"].reshape(3, -1).T,
        "L2_W_T": a["L2_gnn_W"].T, "L2_b": a["L2_gnn_b"].reshape(1, -1),
        "L3_eps": a["L3_gnn_eps"].reshape(1, 1), "L3_W1": a["L3_gnn_W1"],
        "L3_b1": a["L3_gnn_b1"].reshape(2, -1).T, "L3_W2": a["L3_gnn_W2"],
        "L3_b2": a["L3_gnn_b2"].reshape(1, -1),
    }
    nc = bacc.Bacc("TRN2", target_bir_lowering=False, num_devices=1)
    arrays, aps = {}, {}
    for name, v in lay.items():
        v = np.ascontiguousarray(v)
        arrays[f"in_{name}"] = v
        aps[name] = nc.dram_tensor(f"in_{name}", v.shape, mybir.dt.from_np(v.dtype), kind="ExternalInput").ap()
    out = nc.dram_tensor("out", a["x"].shape, F32, kind="ExternalOutput").ap()
    gnn_stack(nc, aps, out)
    r = run_bass_kernel_spmd(nc, [arrays], core_ids=[0])
    return r.results[0]["out"]
```
